# Optimizing a Trainium2 kernel written in Bass

```python
import numpy as np
import jax
import jax.numpy as jnp

def _softmax(x, axis=-1):
    return jax.nn.softmax(x, axis=axis)

def _gelu(x):
    return jax.nn.gelu(x, approximate=True)

def _silu(x):
    return jax.nn.silu(x)

def _sigmoid(x):
    return jax.nn.sigmoid(x)

def _layernorm(x, axis=-1, eps=1e-05):
    m = jnp.mean(x, axis=axis, keepdims=True)
    v = jnp.var(x, axis=axis, keepdims=True)
    return (x - m) / jnp.sqrt(v + eps)

def _scatter_add(tgt, idx, src, axis=0):
    return tgt.at[idx].add(src)

def _segment_sum(src, seg, n):
    return jax.ops.segment_sum(src, seg, n)
kernel_name = 'mk_decoder_preln_d2_seqx_r4_0b3fae'

def setup_inputs(seed: int=0):
    np.random.seed(seed)
    _w = jnp.asarray

    def _rec_inputs():
        import jax
        import jax.numpy as jnp
        _rk = jax.random.key(seed)
        x = 7.22e-05 + 1 * jax.random.normal(jax.random.fold_in(_rk, 1), (4, 512, 256), jnp.float32)
        _lenS = 512 - jax.random.randint(jax.random.fold_in(_rk, 7), (4,), 0, max(1, 512 // 4) + 1, jnp.int32)
        _lenS2 = 1601 - jax.random.randint(jax.random.fold_in(_rk, 8), (4,), 0, max(1, 1601 // 4) + 1, jnp.int32)
        _ctx_768P = jax.random.normal(jax.random.fold_in(_rk, 11), (4, 16, 192), jnp.float32)
        _ctx_768c = jax.random.dirichlet(jax.random.fold_in(_rk, 511), 0.3 * jnp.ones((16,), jnp.float32), (4, 1601))
        _ctx_768t = jnp.einsum('bsk,bkd->bsd', _ctx_768c, _ctx_768P)
        _ctx_768t = _ctx_768t * jax.lax.rsqrt(jnp.mean(jnp.square(_ctx_768t)) + 1e-12) * 0.953939
        ctx_768 = -0.000191848 + 0.999787 * (_ctx_768t + 0.3 * jax.random.normal(jax.random.fold_in(_rk, 611), (4, 1601, 192), jnp.float32))
        _validS = jnp.arange(512)[None, :] < _lenS[:, None]
        _validS2 = jnp.arange(1601)[None, :] < _lenS2[:, None]
        _causal = jnp.tril(jnp.ones((512, 512), dtype=bool))
        mask_BxS2_bk0 = jnp.logical_not(jnp.broadcast_to(_validS2[:, :], (4, 1601)))
        return (x, ctx_768, mask_BxS2_bk0)
    x, ctx_768, mask_BxS2_bk0 = _rec_inputs()

    def _L0_attn_setup():
        import jax, jax.numpy as jnp
        import numpy as np
        import math
        NUM_HEADS = 16
        MAX_BIAS = 8.0

        def _alibi_slopes(n_heads):

            def slopes(n):
                start = 2.0 ** (-2 ** (-(math.log2(n) - 3)))
                return [start * start ** i for i in range(n)]
            if math.log2(n_heads).is_integer():
                s = slopes(n_heads)
            else:
                p = 2 ** math.floor(math.log2(n_heads))
                s = slopes(p) + slopes(2 * p)[0::2][:n_heads - p]
            return jnp.asarray(np.array(s, dtype=np.float32))
        key = jax.random.key(seed)
        ks = jax.random.split(key, 5)
        B, S, C = (2, 512, 256)
        return {'x': jax.random.normal(ks[0], (B, S, C), jnp.float32), 'in_proj_weight': jax.random.normal(ks[1], (3 * C, C), jnp.float32) * C ** (-0.5), 'in_proj_bias': jax.random.normal(ks[2], (3 * C,), jnp.float32) * 0.02, 'out_proj_weight': jax.random.normal(ks[3], (C, C), jnp.float32) * C ** (-0.5), 'out_proj_bias': jax.random.normal(ks[4], (C,), jnp.float32) * 0.02}
    _L0_attn_all = _L0_attn_setup()
    _L0_attn_in = {k: v for k, v in _L0_attn_all.items() if k in ('in_proj_weight', 'in_proj_bias', 'out_proj_weight', 'out_proj_bias')}
    del _L0_attn_all

    def _L0_xattn_setup():
        import jax, jax.numpy as jnp
        import numpy as np
        HEADS = 8
        DIM_HEAD = 64
        QUERY_DIM = 256
        CONTEXT_DIM = 192
        INNER = HEADS * DIM_HEAD
        key = jax.random.key(seed)
        ks = jax.random.split(key, 8)
        b, n, j = (4, 512, 512)
        x = jax.random.normal(ks[0], (b, n, QUERY_DIM), dtype=jnp.float32)
        context = jax.random.normal(ks[1], (b, j, CONTEXT_DIM), dtype=jnp.float32)
        mask = jax.random.randint(ks[2], (b, j), 0, 2).astype(jnp.bool_)
        W_q = jax.random.normal(ks[3], (QUERY_DIM, INNER), dtype=jnp.float32) / np.sqrt(QUERY_DIM)
        W_k = jax.random.normal(ks[4], (CONTEXT_DIM, INNER), dtype=jnp.float32) / np.sqrt(CONTEXT_DIM)
        W_v = jax.random.normal(ks[5], (CONTEXT_DIM, INNER), dtype=jnp.float32) / np.sqrt(CONTEXT_DIM)
        W_o = jax.random.normal(ks[6], (INNER, QUERY_DIM), dtype=jnp.float32) / np.sqrt(INNER)
        b_o = jax.random.normal(ks[7], (QUERY_DIM,), dtype=jnp.float32) * 0.01
        return {'x': x, 'context': context, 'mask': mask, 'W_q': W_q, 'W_k': W_k, 'W_v': W_v, 'W_o': W_o, 'b_o': b_o}
    _L0_xattn_all = _L0_xattn_setup()
    _L0_xattn_in = {k: v for k, v in _L0_xattn_all.items() if k in ('W_q', 'W_k', 'W_v', 'W_o', 'b_o')}
    del _L0_xattn_all

    def _L0_ffn_setup():
        import jax, jax.numpy as jnp
        import numpy as np
        B, L, H = (8, 512, 256)
        E, K, R = (8, 2, 64)

        def _gates(cls_tok, Wr):
            logits = cls_tok @ Wr.T
            top_vals, top_idx = jax.lax.top_k(logits, K)
            neg_inf = jnp.full_like(logits, -jnp.inf)
            rows = jnp.arange(logits.shape[0])[:, None]
            masked = neg_inf.at[rows, top_idx].set(top_vals)
            return jax.nn.softmax(masked, axis=-1)
        key = jax.random.key(seed)
        k1, k2, k3, k4 = jax.random.split(key, 4)
        x = jax.random.normal(k1, (B, L, H), dtype=jnp.float32)
        Wr = jax.random.normal(k2, (E, H), dtype=jnp.float32) * (1.0 / np.sqrt(H))
        A = jax.random.normal(k3, (E, R, H), dtype=jnp.float32) * (1.0 / np.sqrt(H))
        Bw = jax.random.normal(k4, (E, H, R), dtype=jnp.float32) * (1.0 / np.sqrt(R))
        return {'x': x, 'Wr': Wr, 'A': A, 'Bw': Bw}
    _L0_ffn_all = _L0_ffn_setup()
    _L0_ffn_in = {k: v for k, v in _L0_ffn_all.items() if k in ('Wr', 'A', 'Bw')}
    del _L0_ffn_all

    def _L1_attn_setup():
        import jax, jax.numpy as jnp
        import numpy as np
        S, B, E, H = (512, 2, 256, 16)
        D = E // H
        key = jax.random.key(seed)
        ks = jax.random.split(key, 8)
        x = jax.random.normal(ks[0], (S, B, E), dtype=jnp.float32)
        in_proj_weight = jax.random.normal(ks[1], (3 * E, E), dtype=jnp.float32) * 0.02
        in_proj_bias = jax.random.normal(ks[2], (3 * E,), dtype=jnp.float32) * 0.02
        gamma = 1.0 + jax.random.normal(ks[3], (1, 1, 3 * E), dtype=jnp.float32) * 0.1
        linear_alpha = 1.0 + jax.random.normal(ks[4], (1, 1, E), dtype=jnp.float32) * 0.1
        linear_gamma = 1.0 + jax.random.normal(ks[5], (1, 1, E), dtype=jnp.float32) * 0.1
        out_proj_weight = jax.random.normal(ks[6], (E, E), dtype=jnp.float32) * 0.02
        out_proj_bias = jax.random.normal(ks[7], (E,), dtype=jnp.float32) * 0.02
        return {'x': x, 'in_proj_weight': in_proj_weight, 'in_proj_bias': in_proj_bias, 'gamma': gamma, 'linear_alpha': linear_alpha, 'linear_gamma': linear_gamma, 'out_proj_weight': out_proj_weight, 'out_proj_bias': out_proj_bias}
    _L1_attn_all = _L1_attn_setup()
    _L1_attn_in = {k: v for k, v in _L1_attn_all.items() if k in ('in_proj_weight', 'in_proj_bias', 'gamma', 'linear_alpha', 'linear_gamma', 'out_proj_weight', 'out_proj_bias')}
    del _L1_attn_all

    def _L1_xattn_setup():
        import jax, jax.numpy as jnp
        import numpy as np
        HEADS = 16
        DIM_HEAD = 64
        key = jax.random.key(seed)
        ks = jax.random.split(key, 8)
        B, S, D = (16, 1024, 256)
        K, DE = (77, 192)
        inner = HEADS * DIM_HEAD
        hidden_states = jax.random.normal(ks[0], (B, S, D), dtype=jnp.float32)
        encoder_hidden_states = jax.random.normal(ks[1], (B, K, DE), dtype=jnp.float32)
        sc_q = 1.0 / np.sqrt(D)
        sc_kv = 1.0 / np.sqrt(DE)
        sc_o = 1.0 / np.sqrt(inner)
        Wq = jax.random.normal(ks[2], (D, inner), dtype=jnp.float32) * sc_q
        Wk = jax.random.normal(ks[3], (DE, inner), dtype=jnp.float32) * sc_kv
        Wv = jax.random.normal(ks[4], (DE, inner), dtype=jnp.float32) * sc_kv
        Wo = jax.random.normal(ks[5], (inner, D), dtype=jnp.float32) * sc_o
        bo = jax.random.normal(ks[6], (D,), dtype=jnp.float32) * 0.01
        return {'hidden_states': hidden_states, 'encoder_hidden_states': encoder_hidden_states, 'Wq': Wq, 'Wk': Wk, 'Wv': Wv, 'Wo': Wo, 'bo': bo}
    _L1_xattn_all = _L1_xattn_setup()
    _L1_xattn_in = {k: v for k, v in _L1_xattn_all.items() if k in ('Wq', 'Wk', 'Wv', 'Wo', 'bo')}
    del _L1_xattn_all

    def _L1_ffn_setup():
        import jax, jax.numpy as jnp
        import numpy as np
        D_MODEL = 256
        HIDDEN = 1024
        NUM_EXPERTS = 8
        TOP_K = 2
        key = jax.random.key(seed)
        k_x, k_g, k_in, k_out = jax.random.split(key, 4)
        bound_in = 1.0 / HIDDEN
        bound_out = 1.0 / D_MODEL
        x = jax.random.normal(k_x, (2, 512, D_MODEL), dtype=jnp.float32)
        w_gate = jax.random.uniform(k_g, (NUM_EXPERTS, D_MODEL), dtype=jnp.float32, minval=-D_MODEL ** (-0.5), maxval=D_MODEL ** (-0.5))
        w_in = jax.random.uniform(k_in, (NUM_EXPERTS, HIDDEN, D_MODEL), dtype=jnp.float32, minval=-bound_in, maxval=bound_in)
        w_out = jax.random.uniform(k_out, (NUM_EXPERTS, D_MODEL, HIDDEN), dtype=jnp.float32, minval=-bound_out, maxval=bound_out)
        return {'x': x, 'w_gate': w_gate, 'w_in': w_in, 'w_out': w_out}
    _L1_ffn_all = _L1_ffn_setup()
    _L1_ffn_in = {k: v for k, v in _L1_ffn_all.items() if k in ('w_gate', 'w_in', 'w_out')}
    del _L1_ffn_all
    return {'x': x, 'ctx_768': ctx_768, 'mask_BxS2_bk0': mask_BxS2_bk0, 'L0_attn_in_proj_weight': _L0_attn_in['in_proj_weight'], 'L0_attn_in_proj_bias': _L0_attn_in['in_proj_bias'], 'L0_attn_out_proj_weight': _L0_attn_in['out_proj_weight'], 'L0_attn_out_proj_bias': _L0_attn_in['out_proj_bias'], 'L0_xattn_W_q': _L0_xattn_in['W_q'], 'L0_xattn_W_k': _L0_xattn_in['W_k'], 'L0_xattn_W_v': _L0_xattn_in['W_v'], 'L0_xattn_W_o': _L0_xattn_in['W_o'], 'L0_xattn_b_o': _L0_xattn_in['b_o'], 'L0_ffn_Wr': _L0_ffn_in['Wr'], 'L0_ffn_A': _L0_ffn_in['A'], 'L0_ffn_Bw': _L0_ffn_in['Bw'], 'L1_attn_in_proj_weight': _L1_attn_in['in_proj_weight'], 'L1_attn_in_proj_bias': _L1_attn_in['in_proj_bias'], 'L1_attn_gamma': _L1_attn_in['gamma'], 'L1_attn_linear_alpha': _L1_attn_in['linear_alpha'], 'L1_attn_linear_gamma': _L1_attn_in['linear_gamma'], 'L1_attn_out_proj_weight': _L1_attn_in['out_proj_weight'], 'L1_attn_out_proj_bias': _L1_attn_in['out_proj_bias'], 'L1_xattn_Wq': _L1_xattn_in['Wq'], 'L1_xattn_Wk': _L1_xattn_in['Wk'], 'L1_xattn_Wv': _L1_xattn_in['Wv'], 'L1_xattn_Wo': _L1_xattn_in['Wo'], 'L1_xattn_bo': _L1_xattn_in['bo'], 'L1_ffn_w_gate': _L1_ffn_in['w_gate'], 'L1_ffn_w_in': _L1_ffn_in['w_in'], 'L1_ffn_w_out': _L1_ffn_in['w_out']}

def reference(x, ctx_768, mask_BxS2_bk0, L0_attn_in_proj_weight, L0_attn_in_proj_bias, L0_attn_out_proj_weight, L0_attn_out_proj_bias, L0_xattn_W_q, L0_xattn_W_k, L0_xattn_W_v, L0_xattn_W_o, L0_xattn_b_o, L0_ffn_Wr, L0_ffn_A, L0_ffn_Bw, L1_attn_in_proj_weight, L1_attn_in_proj_bias, L1_attn_gamma, L1_attn_linear_alpha, L1_attn_linear_gamma, L1_attn_out_proj_weight, L1_attn_out_proj_bias, L1_xattn_Wq, L1_xattn_Wk, L1_xattn_Wv, L1_xattn_Wo, L1_xattn_bo, L1_ffn_w_gate, L1_ffn_w_in, L1_ffn_w_out):
    import jax
    import jax.numpy as jnp

    def _L0_attn_ref(x, in_proj_weight, in_proj_bias, out_proj_weight, out_proj_bias):
        import jax, jax.numpy as jnp
        import numpy as np
        import math
        NUM_HEADS = 16
        MAX_BIAS = 8.0

        def _alibi_slopes(n_heads):

            def slopes(n):
                start = 2.0 ** (-2 ** (-(math.log2(n) - 3)))
                return [start * start ** i for i in range(n)]
            if math.log2(n_heads).is_integer():
                s = slopes(n_heads)
            else:
                p = 2 ** math.floor(math.log2(n_heads))
                s = slopes(p) + slopes(2 * p)[0::2][:n_heads - p]
            return jnp.asarray(np.array(s, dtype=np.float32))
        B, S, C = x.shape
        H = NUM_HEADS
        D = C // H
        qkv = x @ in_proj_weight.T + in_proj_bias
        qkv = qkv.reshape(B, S, 3, H, D).transpose(2, 0, 3, 1, 4)
        q, k, v = (qkv[0], qkv[1], qkv[2])
        slopes = _alibi_slopes(H)
        pos = jnp.arange(S, dtype=jnp.float32)
        rel = pos[:, None] - pos[None, :]
        bias = jnp.minimum(rel[None, :, :] * slopes[:, None, None], MAX_BIAS)
        scores = jnp.einsum('bhqd,bhkd->bhqk', q, k) * D ** (-0.5) + bias[None]
        probs = jax.nn.softmax(scores, axis=-1)
        out = jnp.einsum('bhqk,bhkd->bhqd', probs, v)
        out = out.transpose(0, 2, 1, 3).reshape(B, S, C)
        return out @ out_proj_weight.T + out_proj_bias

    def _L0_xattn_ref(x, context, mask, W_q, W_k, W_v, W_o, b_o):
        import jax, jax.numpy as jnp
        import numpy as np
        HEADS = 8
        DIM_HEAD = 64
        QUERY_DIM = 256
        CONTEXT_DIM = 192
        INNER = HEADS * DIM_HEAD
        b, n, _ = x.shape
        j = context.shape[1]
        scale = DIM_HEAD ** (-0.5)
        q = (x @ W_q).reshape(b, n, HEADS, DIM_HEAD)
        k = (context @ W_k).reshape(b, j, HEADS, DIM_HEAD)
        v = (context @ W_v).reshape(b, j, HEADS, DIM_HEAD)
        sim = jnp.einsum('bihd,bjhd->bhij', q, k) * scale
        max_neg = -jnp.finfo(sim.dtype).max
        sim = jnp.where(mask[:, None, None, :], sim, max_neg)
        attn = jax.nn.softmax(sim, axis=-1)
        out = jnp.einsum('bhij,bjhd->bihd', attn, v).reshape(b, n, INNER)
        return out @ W_o + b_o

    def _L0_ffn_ref(x, Wr, A, Bw):
        import jax, jax.numpy as jnp
        import numpy as np
        B, L, H = (8, 512, 256)
        E, K, R = (8, 2, 64)

        def _gates(cls_tok, Wr):
            logits = cls_tok @ Wr.T
            top_vals, top_idx = jax.lax.top_k(logits, K)
            neg_inf = jnp.full_like(logits, -jnp.inf)
            rows = jnp.arange(logits.shape[0])[:, None]
            masked = neg_inf.at[rows, top_idx].set(top_vals)
            return jax.nn.softmax(masked, axis=-1)
        gates = _gates(x[:, 0, :], Wr)
        mid = jnp.einsum('blh,erh->belr', x, A)
        expert_out = jnp.einsum('belr,ehr->belh', mid, Bw)
        weighted = jnp.einsum('be,belh->blh', gates, expert_out)
        return x + weighted

    def _L1_attn_ref(x, in_proj_weight, in_proj_bias, gamma, linear_alpha, linear_gamma, out_proj_weight, out_proj_bias):
        import jax, jax.numpy as jnp
        import numpy as np
        S, B, E, H = (512, 2, 256, 16)
        D = E // H
        s, b, e = x.shape
        qkv = jnp.einsum('sbe,fe->sbf', x, in_proj_weight) + in_proj_bias
        qkv = qkv * gamma
        q, k, v = jnp.split(qkv, 3, axis=-1)

        def to_heads(t):
            return t.reshape(s, b * H, D).transpose(1, 0, 2)
        q, k, v = (to_heads(q), to_heads(k), to_heads(v))
        q = q / jnp.sqrt(jnp.asarray(D, dtype=q.dtype))
        scores = jnp.einsum('bsd,btd->bst', q, k)
        causal = jnp.tril(jnp.ones((s, s), dtype=bool))
        scores = jnp.where(causal[None], scores, jnp.asarray(-jnp.inf, scores.dtype))
        attn = jax.nn.softmax(scores, axis=-1)
        out = jnp.einsum('bst,btd->bsd', attn, v)
        out = out.transpose(1, 0, 2).reshape(s, b, e)
        out = out * linear_alpha
        out = jnp.einsum('sbe,fe->sbf', out, out_proj_weight) + out_proj_bias
        out = out * linear_gamma
        return out

    def _L1_xattn_ref(hidden_states, encoder_hidden_states, Wq, Wk, Wv, Wo, bo):
        import jax, jax.numpy as jnp
        import numpy as np
        HEADS = 16
        DIM_HEAD = 64
        B, S, D = hidden_states.shape
        K = encoder_hidden_states.shape[1]
        H, Dh = (HEADS, DIM_HEAD)
        scale = 1.0 / np.sqrt(Dh)
        q = hidden_states @ Wq
        k = encoder_hidden_states @ Wk
        v = encoder_hidden_states @ Wv
        q = q.reshape(B, S, H, Dh).transpose(0, 2, 1, 3)
        k = k.reshape(B, K, H, Dh).transpose(0, 2, 1, 3)
        v = v.reshape(B, K, H, Dh).transpose(0, 2, 1, 3)
        scores = jnp.einsum('bhsd,bhkd->bhsk', q, k) * scale
        probs = jax.nn.softmax(scores, axis=-1)
        out = jnp.einsum('bhsk,bhkd->bhsd', probs, v)
        out = out.transpose(0, 2, 1, 3).reshape(B, S, H * Dh)
        out = out @ Wo + bo
        return out

    def _L1_ffn_ref(x, w_gate, w_in, w_out):
        import jax, jax.numpy as jnp
        import numpy as np
        D_MODEL = 256
        HIDDEN = 1024
        NUM_EXPERTS = 8
        TOP_K = 2
        B, S, D = x.shape
        E = w_in.shape[0]
        xt = x.reshape(-1, D)
        logits = (xt @ w_gate.T).astype(jnp.float32)
        top_logits, top_idx = jax.lax.top_k(logits, TOP_K)
        top_gates = jax.nn.softmax(top_logits, axis=-1).astype(x.dtype)
        gates = (jax.nn.one_hot(top_idx, E, dtype=x.dtype) * top_gates[..., None]).sum(axis=1)
        y = jnp.zeros_like(xt)
        for e in range(E):
            h = xt @ w_in[e].T
            y = y + gates[:, e:e + 1] * (h @ w_out[e].T)
        return y.reshape(B, S, D)
    x = x + _L0_attn_ref(_layernorm(x, axis=-1), L0_attn_in_proj_weight, L0_attn_in_proj_bias, L0_attn_out_proj_weight, L0_attn_out_proj_bias)
    x = x + _L0_xattn_ref(_layernorm(x, axis=-1), ctx_768, mask_BxS2_bk0, L0_xattn_W_q, L0_xattn_W_k, L0_xattn_W_v, L0_xattn_W_o, L0_xattn_b_o)
    x = x + _L0_ffn_ref(_layernorm(x, axis=-1), L0_ffn_Wr, L0_ffn_A, L0_ffn_Bw)
    x = x + _L1_attn_ref(_layernorm(x, axis=-1), L1_attn_in_proj_weight, L1_attn_in_proj_bias, L1_attn_gamma, L1_attn_linear_alpha, L1_attn_linear_gamma, L1_attn_out_proj_weight, L1_attn_out_proj_bias)
    x = x + _L1_xattn_ref(_layernorm(x, axis=-1), ctx_768, L1_xattn_Wq, L1_xattn_Wk, L1_xattn_Wv, L1_xattn_Wo, L1_xattn_bo)
    x = x + _L1_ffn_ref(_layernorm(x, axis=-1), L1_ffn_w_gate, L1_ffn_w_in, L1_ffn_w_out)
    return x

_drawn_inputs = setup_inputs


def setup_inputs(seed=0):
    import zlib

    import numpy as np

    out = dict(_drawn_inputs(seed))
    spreads = {}
    factors = {'L0_attn_out_proj_bias': 3.401,
     'L0_xattn_b_o': 6.552,
     'L1_attn_in_proj_bias': 8.0,
     'L1_attn_gamma': 8.0,
     'L1_attn_linear_alpha': 8.0,
     'L1_attn_linear_gamma': 8.0,
     'L1_attn_out_proj_bias': 20.423,
     'L1_xattn_bo': 200.0,
     'L1_ffn_w_gate': 64.0,
     'L1_ffn_w_in': 64.0,
     'L1_ffn_w_out': 64.0,
     'L1_xattn_Wq': 8.0,
     'L1_xattn_Wk': 8.0,
     'L1_xattn_Wv': 6.428,
     'L1_xattn_Wo': 6.282}
    for name, (base, spread) in spreads.items():
        noise = np.random.default_rng([zlib.crc32(name.encode()), seed]).standard_normal(out[name].shape)
        drawn = base * np.exp(spread * noise) if base else spread * noise
        out[name] = jnp.asarray(drawn.astype(out[name].dtype))
    for name, factor in factors.items():
        out[name] = (out[name] * factor).astype(out[name].dtype)
    return out
```

```python
from contextlib import ExitStack, contextmanager

import concourse.bass as bass
from concourse import mybir

F32 = mybir.dt.float32
F32R = mybir.dt.float32r
U8 = mybir.dt.uint8
ALU = mybir.AluOpType
ACT = mybir.ActivationFunctionType
AX = mybir.AxisListType

P = 128
B, S, C = 4, 512, 256
NT = S // P
CK = C // P
H, D = 16, 16
S2, CC = 1601, 192
S2E = S2 + S2 % 2
KT = -(-S2 // P)
TAIL = S2 - (KT - 1) * P
DH = 64
E0, R0 = 8, 64
E1, F1 = 8, 1024
EPS = 1e-5
BIG = 3e38
CHUNKS = [(0, 400), (400, 400), (800, 400), (1200, S2E - 1200)]
NC = len(CHUNKS)
VG = [(0, 4), (4, 4), (8, 4), (12, KT - 12)]


def rows_of(kt):
    return P if kt < KT - 1 else TAIL


def raw(ap):
    return ap.bitcast(F32)


class Core:

    def __init__(self, nc, ctx, a, out):
        self.nc, self.a, self.out, self.stages = nc, a, out, 0

        self.x_out = ctx.enter_context(nc.semaphore("x_out"))

        def sb(name, shape, dt=F32):
            return ctx.enter_context(nc.sbuf_tensor(name, shape, dt))

        self.X = sb("X", [P, B * NT, C])
        self.Hn = sb("Hn", [P, NT, C])
        self.HT = sb("HT", [P, CK, S])
        self.ident = sb("ident", [P, P])
        self.stats = sb("stats", [P, NT, 6])
        self.mv = sb("mv", [P, NT, 2])
        self.std = sb("std", [P, NT])
        self.rstd = sb("rstd", [P, NT])
        self.KA = sb("KA", [P, 2, 2, S2E], F32R)
        self.KB = sb("KB", [DH + 1, 2, 2, S2E], F32R)
        self.QA = sb("QA", [P, 2, 2, S], F32R)
        self.QB = sb("QB", [DH + 1, 2, 2, S], F32R)
        self.V = sb("V", [P, 2, KT, 2, DH + 1])
        self.PR = sb("PR", [P, 4, S])
        self.On = sb("On", [P, 2, NT, P])
        self.OT = sb("OT", [P, 1024])
        self.C0 = sb("C0", [P, S2E])
        self.C1 = sb("C1", [CC - P, S2E])
        self.W = sb("W", [P, 8192])
        self.HI = sb("HI", [P, 4, S], F32R)
        self.LO = sb("LO", [P, 4, S], F32R)
        self.SK1 = sb("SK1", [P, 8 * S], F32R)
        self.SV = sb("SV", [P, NT, H, D + 1])
        self.bias = sb("bias", [P, 3 * C])
        self.mx = sb("mx", [P, 2, NT, NC])
        self.m4 = sb("m4", [P, 2, NT])
        self.rec = sb("rec", [P, 2, NT])
        self.small = sb("small", [P, 512])
        self.tri = sb("tri", [P, E1, E1])
        self.ones = sb("ones", [P, P])
        self.HTs = self.OT
        self.bank = [ctx.enter_context(nc.psum_tensor(f"bank{i}", [P, 512], F32)) for i in range(8)]

    @contextmanager
    def stage(self):
        nc, names = self.nc, []
        self.stages += 1

        def sem(name):
            names.append(nc.alloc_semaphore(f"{name}_{self.stages}"))
            return names[-1]

        with ExitStack() as ctx:
            yield sem, ctx
        nc.clear_and_free_semaphores(names)
        nc.all_engine_barrier()

    def load_inputs(self):
        nc, a = self.nc, self.a
        with self.stage() as (sem, ctx):
            x_in, zeroed, made = sem("x_in"), sem("zeroed"), sem("made")
            block = ctx.enter_context(nc.Block())

            @block.sync
            def _(sp):
                sp.dma_start(self.X[:, :, :], a["x"].rearrange("b (t p) c -> p (b t) c", p=P)).then_inc(x_in, 16)
                sp.wait_ge(x_in, 16)

            @block.gpsimd
            def _(pool):
                pool.memset(self.ident[:, :], 0.0).then_inc(zeroed, 1)
                pool.wait_ge(zeroed, 1)
                pool.affine_select(out=self.ident[:, :], in_=self.ident[:, :], compare_op=ALU.not_equal, fill=1.0,
                                   base=0, pattern=[[-1, P]], channel_multiplier=1).then_inc(made, 1)
                pool.memset(self.ones[:, :], 1.0).then_inc(made, 1)
                pool.memset(self.tri[:, :, :], 1.0).then_inc(zeroed, 1)
                pool.wait_ge(zeroed, 2)
                pool.affine_select(out=self.tri[:, :, :], in_=self.tri[:, :, :], compare_op=ALU.is_gt, fill=0.0,
                                   base=0, pattern=[[1, E1], [-1, E1]], channel_multiplier=0).then_inc(made, 1)
                pool.memset(self.C0[:, S2:S2E], 0.0).then_inc(made, 1)
                pool.memset(self.C1[:, S2:S2E], 0.0).then_inc(made, 1)

    def cross_constants(self):
        nc = self.nc
        with self.stage() as (sem, ctx):
            made = sem("ones_made")
            block = ctx.enter_context(nc.Block())

            @block.vector
            def _(dve):
                dve.memset(self.small[DH:DH + 1, :], 1.0).then_inc(made, 1)
                dve.memset(self.V[:, :, :, :, DH:DH + 1].rearrange("p a k h o -> p (a k h) o"), 1.0).then_inc(made, 1)
                dve.wait_ge(made, 2)
                dve.memset(self.SV[:, :, :, D:D + 1].rearrange("p t h o -> p (t h) o"), 1.0).then_inc(made, 1)
                for par in range(2):
                    for a in range(2):
                        for o, w in CHUNKS:
                            dve.tensor_copy(self.KB[DH:DH + 1, par, a, o:o + w], self.small[DH:DH + 1, 0:w]).then_inc(made, 1)

    def store_outputs(self):
        nc = self.nc
        with ExitStack() as ctx:
            x_out = self.x_out
            block = ctx.enter_context(nc.Block())

            @block.sync
            def _(sp):
                sp.dma_start(self.out.rearrange("b (t p) c -> p (b t) c", p=P), self.X[:, :, :]).then_inc(x_out, 16)
                sp.wait_ge(x_out, 16)

    def norm(self, b):
        nc = self.nc
        X, Hn, HT = self.X, self.Hn, self.HT
        with self.stage() as (sem, ctx):
            step, var_ready, std_ready, rows_ready, turned = (
                sem("n_step"), sem("n_var"), sem("n_std"), sem("n_rows"), sem("n_turned"))
            block = ctx.enter_context(nc.Block())

            @block.vector
            def _(dve):
                for t in range(NT):
                    dve.bn_stats(self.stats[:, t, :], X[:, b * NT + t, :]).then_inc(step, 1)
                dve.wait_ge(step, NT)
                for t in range(NT):
                    dve.bn_aggr(self.mv[:, t, :], self.stats[:, t, :]).then_inc(step, 1)
                dve.wait_ge(step, 2 * NT)
                dve.tensor_scalar(self.std[:, :], self.mv[:, :, 1], EPS, None, ALU.add).then_inc(var_ready, 1)
                dve.wait_ge(std_ready, 1)
                dve.reciprocal(self.rstd[:, :], self.rstd[:, :]).then_inc(step, 1)
                dve.wait_ge(step, 2 * NT + 1)
                for t in range(NT):
                    dve.tensor_scalar(Hn[:, t, :], X[:, b * NT + t, :], self.mv[:, t, 0:1], self.rstd[:, t:t + 1],
                                      ALU.subtract, ALU.mult).then_inc(rows_ready, 1)
                dve.wait_ge(turned, 2)
                dve.tensor_copy(HT[:, 1, :], self.bank[1][:, :]).then_inc(step, 1)

            @block.scalar
            def _(act):
                act.wait_ge(var_ready, 1)
                act.activation(self.rstd[:, :], self.std[:, :], ACT.Sqrt).then_inc(std_ready, 1)
                act.wait_ge(turned, 1)
                act.activation(HT[:, 0, :], self.bank[0][:, :], ACT.Copy).then_inc(std_ready, 1)

            @block.tensor
            def _(pe):
                pe.wait_ge(rows_ready, NT)
                for k in range(CK):
                    for t in range(NT):
                        last = pe.transpose(self.bank[k][:, t * P:(t + 1) * P], Hn[:, t, k * P:(k + 1) * P], self.ident[:, :])
                    last.then_inc(turned, 1)

    def stacked(self, h, keys):
        if h < 8:
            t = self.KB if keys else self.KA
            flat = t[:, :, :, :].rearrange("p a h n -> p (a h n)")
            return flat[0:3 * D + 1, h * S:(h + 1) * S]
        if keys:
            return self.SK1[0:3 * D + 1, (h - 8) * S:(h - 7) * S]
        t = self.QA if h < 12 else self.QB
        return t[:, :, :, :].rearrange("p a h n -> p (a h n)")[0:3 * D + 1, (h % 4) * S:(h % 4 + 1) * S]

    def self_project(self, b):
        nc, a, HT, bank = self.nc, self.a, self.HT, self.bank
        w = self.W[:, 0:CK * 3 * C].rearrange("p (k n) -> p k n", k=CK)
        full = self.W[:, 2048:3072].rearrange("p (r n) -> p r n", r=2)
        bcol = self.W[:, 3072:3076]
        vbias = self.bias[:, 0:C]
        HI, LO = self.HI, self.LO
        with self.stage() as (sem, ctx):
            w_in, b_in, ones, q_ready, full_ready, hi_ready, lo_ready, v_done, stacked = (
                sem("sp_w"), sem("sp_b"), sem("sp_ones"), sem("sp_q"), sem("sp_full"), sem("sp_hi"), sem("sp_lo"),
                sem("sp_v"), sem("sp_stacked"))
            block = ctx.enter_context(nc.Block())

            @block.sync
            def _(sp):
                sp.dma_start(w, a["w0_in"].rearrange("(k p) n -> p k n", p=P)).then_inc(w_in, 16)
                sp.dma_start(bcol, a["b0_cols"]).then_inc(b_in, 16)
                sp.dma_start(vbias, a["b0_in"][2 * C:3 * C].partition_broadcast(P)).then_inc(b_in, 16)
                n = 0
                for i in (0, 2, 1, 3):
                    keys, g = i // 2, i % 2
                    sp.wait_ge(lo_ready, i + 1)
                    for r in range(8):
                        dst = self.stacked(8 * g + r, keys)
                        src = slice(D * r, D * (r + 1))
                        second = HI if keys else LO
                        third = LO if keys else HI
                        sp.dma_start(raw(dst[0:D]), raw(HI[src, i, :])).then_inc(stacked, 16)
                        sp.dma_start(raw(dst[D:2 * D]), raw(second[src, i, :])).then_inc(stacked, 16)
                        sp.dma_start(raw(dst[2 * D + 1:3 * D + 1]), raw(third[src, i, :])).then_inc(stacked, 16)
                        n += 3
                sp.wait_ge(stacked, 16 * n)

            @block.gpsimd
            def _(pool):
                for h in range(H):
                    pool.memset(raw(self.stacked(h, True)[2 * D:2 * D + 1]), 1.0).then_inc(ones, 1)

            @block.tensor
            def _(pe):
                pe.wait_ge(w_in, 16)
                for i in range(4):
                    if i >= 2:
                        pe.wait_ge(full_ready, i - 1)
                    for k in range(CK):
                        last = pe.matmul(bank[i % 2][:, :], w[:, k, i * P:(i + 1) * P], HT[:, k, :],
                                         start=(k == 0), stop=(k == CK - 1))
                    last.then_inc(q_ready, 1)
                for t in range(NT):
                    for k in range(CK):
                        last = pe.matmul(bank[2 + t][:, 0:C], HT[:, k, t * P:(t + 1) * P], w[:, k, 2 * C:3 * C],
                                         start=(k == 0), stop=(k == CK - 1))
                    last.then_inc(q_ready, 1)

            @block.scalar
            def _(act):
                for i in range(4):
                    act.wait_ge(full_ready, i + 1)
                    act.activation(HI[:, i, :], full[:, i % 2, :], ACT.Copy).then_inc(hi_ready, 1)

            @block.vector
            def _(dve):
                dve.wait_ge(b_in, 32)
                for i in range(5):
                    if i < 4:
                        dve.wait_ge(q_ready, i + 1)
                        if i >= 2:
                            dve.wait_ge(lo_ready, i - 1)
                        dve.tensor_scalar(full[:, i % 2, :], bank[i % 2][:, :], bcol[:, i:i + 1],
                                          D ** -0.5 if i < 2 else 1.0, ALU.add, ALU.mult).then_inc(full_ready, 1)
                    if i >= 1:
                        dve.wait_ge(hi_ready, i)
                        dve.tensor_tensor(LO[:, i - 1, :], full[:, (i - 1) % 2, :], HI[:, i - 1, :],
                                          ALU.subtract).then_inc(lo_ready, 1)
                for t in range(NT):
                    dve.wait_ge(q_ready, 5 + t)
                    dve.tensor_tensor(self.SV[:, t, :, 0:D], bank[2 + t][:, 0:C].rearrange("p (h d) -> p h d", h=H),
                                      vbias.rearrange("p (h d) -> p h d", h=H), ALU.add).then_inc(v_done, 1)

    def self_attend(self, b):
        nc, bank = self.nc, self.bank
        SPAN = S + (NT - 1) * P
        relq = self.W[:, 0:SPAN]
        relk = self.W[:, SPAN:2 * SPAN]
        stripq = self.W[:, 2 * SPAN:4 * SPAN].rearrange("p (r x) -> p r x", r=2)
        stripk = self.W[:, 4 * SPAN:6 * SPAN].rearrange("p (r x) -> p r x", r=2)
        PR, V, A, m4, rec, ident = self.PR, self.SV, self.Hn, self.m4, self.rec, self.ident
        slopes = [2.0 ** (-(i + 1) / 2) for i in range(H)]
        N = H * NT
        AHEAD, LAG = 6, 2
        SB, MB, OB, RB = bank[0:3], bank[3:5], bank[5:7], bank[7]
        with self.stage() as (sem, ctx):
            rel, sq_ready, sk_ready, sc_ready, biased, probs, used, mx_ready, mx_done, row_ready, row_done, o_step, o_done = (
                sem("sa_rel"), sem("sa_sq"), sem("sa_sk"), sem("sa_scores"), sem("sa_biased"), sem("sa_probs"),
                sem("sa_used"), sem("sa_mxready"), sem("sa_mxdone"), sem("sa_rowready"), sem("sa_rowdone"),
                sem("sa_ostep"), sem("sa_odone"))
            block = ctx.enter_context(nc.Block())

            @block.gpsimd
            def _(pool):
                pool.iota(relq, [[-1, SPAN]], base=(NT - 1) * P, channel_multiplier=1,
                          allow_small_or_imprecise_dtypes=True).then_inc(rel, 1)
                pool.iota(relk, [[1, SPAN]], base=-(NT - 1) * P, channel_multiplier=-1,
                          allow_small_or_imprecise_dtypes=True).then_inc(rel, 1)

            @block.tensor
            def _(pe):
                def maxima(m):
                    h, t = m // NT, m % NT
                    if m >= 2:
                        pe.wait_ge(mx_done, m - 1)
                    pe.matmul(MB[m % 2][:, :], self.stacked(h, False)[0:2 * D, t * P:(t + 1) * P],
                              self.stacked(h, True)[0:2 * D, :], start=True, stop=True).then_inc(mx_ready, 1)

                def max_row(h):
                    pe.wait_ge(mx_done, NT * (h + 1))
                    if h >= 1:
                        pe.wait_ge(row_done, h)
                    for t in range(NT):
                        last = pe.matmul(RB[0:1, t * P:(t + 1) * P], m4[:, h % 2, t:t + 1], ident[:, :],
                                         start=True, stop=True)
                    last.then_inc(row_ready, 1)

                for m in range(AHEAD):
                    maxima(m)
                    if m == NT:
                        max_row(0)
                for n in range(N + LAG):
                    if n < N:
                        h, t = n // NT, n % NT
                        if n >= 3:
                            pe.wait_ge(probs, n - 2)
                        if t == 0:
                            pe.wait_ge(row_done, h + 1)
                        pe.matmul(SB[n % 3][:, :], self.stacked(h, True)[:, t * P:(t + 1) * P], self.stacked(h, False),
                                  start=True, stop=True).then_inc(sc_ready, 1)
                        if n % NT == 2 and (n + 2) // NT < H:
                            max_row((n + 2) // NT)
                        if n + AHEAD < N:
                            maxima(n + AHEAD)
                    if n >= LAG:
                        j = n - LAG
                        h, t = j // NT, j % NT
                        pe.wait_ge(probs, j + 1)
                        if t == 0 and h >= 2:
                            pe.wait_ge(o_done, h - 1)
                        for q in range(NT):
                            last = pe.matmul(OB[h % 2][:, q * (D + 1):(q + 1) * (D + 1)], PR[:, j % 4, q * P:(q + 1) * P],
                                             V[:, t, h, :], start=(t == 0 and q == 0), stop=(t == NT - 1),
                                             skip_group_check=True)
                        last.then_inc(used, 1)

            @block.scalar
            def _(act):
                def make_stripq(h):
                    if h >= 2:
                        act.wait_ge(mx_done, NT * (h - 1))
                    act.activation(stripq[:, h % 2, :], relq, ACT.Relu, bias=8.0, scale=-slopes[h]).then_inc(sq_ready, 1)

                def make_stripk(h):
                    if h >= 2:
                        act.wait_ge(biased, NT * (h - 1))
                    act.activation(stripk[:, h % 2, :], relk, ACT.Relu, bias=8.0, scale=-slopes[h]).then_inc(sk_ready, 1)

                def copy_row(h):
                    act.wait_ge(row_ready, h + 1)
                    act.activation(self.stacked(h, False)[2 * D:2 * D + 1, :], RB[0:1, :], ACT.Copy,
                                   scale=-1.0).then_inc(row_done, 1)

                act.wait_ge(rel, 2)
                make_stripq(0)
                make_stripq(1)
                make_stripk(0)
                copy_row(0)
                for n in range(N):
                    if n >= 4:
                        act.wait_ge(used, n - 3)
                    act.wait_ge(biased, n + 1)
                    act.activation(PR[:, n % 4, :], SB[n % 3][:, :], ACT.Exp).then_inc(probs, 1)
                    if n % NT == 2 and (n + 2) // NT < H:
                        copy_row((n + 2) // NT)
                    if n % NT == 0 and n // NT + 2 < H:
                        make_stripq(n // NT + 2)
                    if n % NT == 1 and (n + 3) // NT < H:
                        make_stripk((n + 3) // NT)

            @block.vector
            def _(dve):
                def maxima(m):
                    h, t = m // NT, m % NT
                    dve.wait_ge(mx_ready, m + 1)
                    if t == 0:
                        dve.wait_ge(sq_ready, h + 1)
                        if h >= 2:
                            dve.wait_ge(row_ready, h - 1)
                    dve.tensor_tensor_reduce(MB[m % 2][:, :], MB[m % 2][:, :], stripq[:, h % 2, (NT - 1 - t) * P:(NT - 1 - t) * P + S],
                                             1.0, -BIG, ALU.subtract, ALU.max, m4[:, h % 2, t:t + 1]).then_inc(mx_done, 1)

                def normalise(h):
                    o = OB[h % 2][:, 0:NT * (D + 1)].rearrange("p (t d) -> p t d", t=NT)
                    dve.wait_ge(used, NT * (h + 1))
                    dve.reciprocal(rec[:, h % 2, :], o[:, :, D]).then_inc(o_step, 1)
                    dve.wait_ge(o_step, h + 1)
                    dve.tensor_tensor(A[:, :, h * D:(h + 1) * D], o[:, :, 0:D],
                                      rec[:, h % 2, :].unsqueeze(2).to_broadcast([P, NT, D]), ALU.mult).then_inc(o_done, 1)

                for m in range(AHEAD):
                    maxima(m)
                for n in range(N):
                    h, t = n // NT, n % NT
                    dve.wait_ge(sc_ready, n + 1)
                    if t == 0:
                        dve.wait_ge(sk_ready, h + 1)
                    dve.tensor_tensor(SB[n % 3][:, :], SB[n % 3][:, :], stripk[:, h % 2, (NT - 1 - t) * P:(NT - 1 - t) * P + S],
                                      ALU.subtract).then_inc(biased, 1)
                    if n + AHEAD < N:
                        maxima(n + AHEAD)
                    if n >= 6 and n % NT == 2:
                        normalise((n - 6) // NT)
                normalise(H - 1)

    def project_out(self, b, w_dram, bias_dram, gamma_dram=None):
        nc, a, A, HT, X, bank = self.nc, self.a, self.Hn, self.HT, self.X, self.bank
        w = self.W[:, 0:CK * C].rearrange("p (k n) -> p k n", k=CK)
        bias, gamma = self.bias[:, 0:C], self.bias[:, C:2 * C]
        out = self.On[:, 0, :, :].rearrange("p t n -> p (t n)").rearrange("p (r n) -> p r n", r=2)
        with self.stage() as (sem, ctx):
            w_in, b_in, turned, copied, y_ready, step = (
                sem("po_w"), sem("po_b"), sem("po_turned"), sem("po_copied"), sem("po_y"), sem("po_step"))
            block = ctx.enter_context(nc.Block())

            @block.sync
            def _(sp):
                sp.dma_start(w, w_dram.rearrange("(k p) n -> p k n", p=P)).then_inc(w_in, 16)
                sp.dma_start(bias, bias_dram.partition_broadcast(P)).then_inc(b_in, 16)
                if gamma_dram is not None:
                    sp.dma_start(gamma, gamma_dram.partition_broadcast(P)).then_inc(b_in, 16)

            @block.tensor
            def _(pe):
                for k in range(CK):
                    for t in range(NT):
                        last = pe.transpose(bank[k][:, t * P:(t + 1) * P], A[:, t, k * P:(k + 1) * P], self.ident[:, :])
                    last.then_inc(turned, 1)
                pe.wait_ge(w_in, 16)
                pe.wait_ge(copied, CK)
                for t in range(NT):
                    for k in range(CK):
                        last = pe.matmul(bank[2 + t][:, 0:C], HT[:, k, t * P:(t + 1) * P], w[:, k, :],
                                         start=(k == 0), stop=(k == CK - 1))
                    last.then_inc(y_ready, 1)

            @block.scalar
            def _(act):
                for k in range(CK):
                    act.wait_ge(turned, k + 1)
                    act.activation(HT[:, k, :], bank[k][:, :], ACT.Copy).then_inc(copied, 1)

            @block.vector
            def _(dve):
                dve.wait_ge(b_in, 16 if gamma_dram is None else 32)
                n = 0
                for t in range(NT):
                    x = X[:, b * NT + t, :]
                    dve.wait_ge(y_ready, t + 1)
                    dve.tensor_tensor(out[:, t % 2, :], bank[2 + t][:, 0:C], bias, ALU.add).then_inc(step, 1)
                    n += 1
                    dve.wait_ge(step, n)
                    if gamma_dram is not None:
                        dve.tensor_tensor(out[:, t % 2, :], out[:, t % 2, :], gamma, ALU.mult).then_inc(step, 1)
                        n += 1
                        dve.wait_ge(step, n)
                    dve.tensor_tensor(x, out[:, t % 2, :], x, ALU.add).then_inc(step, 1)
                    n += 1

    def cross_attention(self, b, heads, names, masked):
        nc, a, bank = self.nc, self.a, self.bank
        X, HT, C0, C1 = self.X, self.HT, self.C0, self.C1
        KA, KB, QA, QB, V, PR, On, OT = self.KA, self.KB, self.QA, self.QB, self.V, self.PR, self.On, self.OT
        mx, m4, rec, ident = self.mx, self.m4, self.rec, self.ident
        inner, pairs = heads * DH, heads // 2
        W = self.W
        wq = W[:, 0:CK * inner].rearrange("p (k n) -> p k n", k=CK)
        wk = W[:, 2 * inner:4 * inner].rearrange("p (k n) -> p k n", k=2)
        wv = W[:, 4 * inner:6 * inner].rearrange("p (k n) -> p k n", k=2)
        wo = W[:, 6 * inner:8 * inner].rearrange("p (j n) -> p j n", j=pairs)
        qscale = self.small[:, 0:1]
        keybias = self.small[:, 16:16 + KT]
        maskadd = W[:, 4096:4096 + S2] if masked else None
        mask_rows = W[:, 6000:6000 + (S2 + 3) // 4 + 1].bitcast(U8)[:, 0:S2] if masked else None
        mask_cols = W[:, 6500:6504].bitcast(U8)[:, 0:KT] if masked else None
        SB, MB, OB, JB = bank[0:2], bank[2:4], bank[4:6], bank[6:8]

        def before():
            return [("k", 0, c) for c in range(NC)] + [("q", 0, 0)] + [("v", 0, g) for g in range(len(VG))]

        def at(j, t):
            p, first, jobs = j // 2, j % 2 == 0, []
            if first and p + 1 < pairs:
                if t < NC:
                    jobs.append(("k", p + 1, t))
                if t == NC:
                    jobs.append(("q", p + 1, 0))
            if not first and p + 1 < pairs and t in (1, 2, 3, 4):
                jobs.append(("v", p + 1, t - 1))
            if first and p >= 1 and t in (5, 7, 8):
                jobs.append([("turn", p - 1, 0), ("out", p - 1, 0), ("out", p - 1, 1)][(5, 7, 8).index(t)])
            if t == 11 and j + 1 < heads:
                jobs.append(("row", j + 1, 0))
            return jobs

        after = [("turn", pairs - 1, 0), ("out", pairs - 1, 0), ("out", pairs - 1, 1)]
        order = before() + [("row", 0, 0)] + [x for j in range(heads) for t in range(KT + 1) for x in at(j, t)] + after
        place = {x: i for i, x in enumerate(order)}

        def chunks_at(j, t):
            return range(2 * (t - 1), 2 * t) if 1 <= t <= 8 and j + 1 < heads else ()

        with self.stage() as (sem, ctx):
            w_in, c_in, m_in, bo_in, prep, x_based = (
                sem("x_win"), sem("x_cin"), sem("x_min"), sem("x_boin"), sem("x_prep"), sem("x_based"))
            sc_ready, probs, used, o_step, o_done = (
                sem("x_scores"), sem("x_probs"), sem("x_used"), sem("x_ostep"), sem("x_odone"))
            mx_ready, mx_done, m_ready = sem("x_mxready"), sem("x_mxdone"), sem("x_mready")
            job_ready = [sem("x_job0"), sem("x_job1")]
            job_done = [sem("x_done0"), sem("x_done1")]
            k_high, q_high, k_twice, q_twice = sem("x_khigh"), sem("x_qhigh"), sem("x_ktwice"), sem("x_qtwice")
            block = ctx.enter_context(nc.Block())

            def wait_job(eng, job):
                i = place[job]
                eng.wait_ge(job_done[i % 2], i // 2 + 1)

            @block.sync
            def _(sp):
                sp.dma_start(C0[:, 0:S2], a["ctxT"][b, 0:P, :]).then_inc(c_in, 16)
                sp.dma_start(C1[:, 0:S2], a["ctxT"][b, P:CC, :]).then_inc(c_in, 16)
                sp.dma_start(wk[:, 0, :], a[names[1]][0:P, :]).then_inc(w_in, 16)
                sp.dma_start(wk[0:CC - P, 1, :], a[names[1]][P:CC, :]).then_inc(w_in, 16)
                sp.dma_start(wq, a[names[0]].rearrange("(k p) n -> p k n", p=P)).then_inc(w_in, 16)
                sp.dma_start(wv[:, 0, :], a[names[2]][0:P, :]).then_inc(w_in, 16)
                sp.dma_start(wv[0:CC - P, 1, :], a[names[2]][P:CC, :]).then_inc(w_in, 16)
                sp.dma_start(wo, a[names[3]].rearrange("(j p) n -> p j n", p=P)).then_inc(w_in, 16)
                sp.dma_start(self.bias[:, 0:C], a[names[4]].partition_broadcast(P)).then_inc(bo_in, 16)
                if masked:
                    sp.dma_start(mask_rows, a["mask"][b].partition_broadcast(P)).then_inc(m_in, 16)
                    sp.dma_start(mask_cols, a["maskT"][b]).then_inc(m_in, 16)
                for p in range(pairs):
                    par = p % 2
                    sp.wait_ge(q_high, p + 1)
                    if p >= 2:
                        sp.wait_ge(sc_ready, 2 * KT * (p - 1))
                    sp.dma_start(raw(QB[0:DH, par, 0, :]), raw(QA[0:DH, par, 0, :])).then_inc(q_twice, 16)
                    sp.dma_start(raw(QB[0:DH, par, 1, :]), raw(QA[DH:P, par, 1, :])).then_inc(q_twice, 16)
                    sp.wait_ge(k_high, NC * (p + 1))
                    sp.dma_start(raw(KA[DH:P, par, 0, :]), raw(KA[0:DH, par, 0, :])).then_inc(k_twice, 16)
                    sp.dma_start(raw(KA[0:DH, par, 1, :]), raw(KA[DH:P, par, 1, :])).then_inc(k_twice, 16)

            @block.gpsimd
            def _(pool):
                pool.wait_ge(bo_in, 16)
                for t in range(NT):
                    x = X[:, b * NT + t, :]
                    pool.tensor_tensor(x, x, self.bias[:, 0:C], ALU.add).then_inc(x_based, 1)

            @block.tensor
            def _(pe):
                def job(x):
                    kind, p, c = x
                    i = place[x]
                    J = JB[i % 2]
                    if i >= 2:
                        pe.wait_ge(job_done[i % 2], i // 2)
                    if kind == "k":
                        o, w = CHUNKS[c]
                        pe.matmul(J[:, 0:w], wk[:, 0, p * P:(p + 1) * P], C0[:, o:o + w], start=True, stop=False)
                        last = pe.matmul(J[:, 0:w], wk[0:CC - P, 1, p * P:(p + 1) * P], C1[:, o:o + w], start=False, stop=True)
                    elif kind == "q":
                        for k in range(CK):
                            last = pe.matmul(J[:, :], wq[:, k, p * P:(p + 1) * P], HT[:, k, :], start=(k == 0), stop=(k == CK - 1))
                    elif kind == "v":
                        t0, n = VG[c]
                        for t in range(t0, t0 + n):
                            r, o = rows_of(t), (t - t0) * P
                            pe.matmul(J[0:r, o:o + P], C0[:, t * P:t * P + r], wv[:, 0, p * P:(p + 1) * P], start=True, stop=False)
                            last = pe.matmul(J[0:r, o:o + P], C1[:, t * P:t * P + r], wv[0:CC - P, 1, p * P:(p + 1) * P],
                                             start=False, stop=True)
                    elif kind == "row":
                        pe.wait_ge(m_ready, p + 1)
                        for t in range(NT):
                            last = pe.matmul(J[0:1, t * P:(t + 1) * P], m4[:, p % 2, t:t + 1], ident[:, :], start=True, stop=True)
                    elif kind == "turn":
                        pe.wait_ge(o_done, 2 * p + 2)
                        for t in range(NT):
                            last = pe.transpose(J[:, t * P:(t + 1) * P], On[:, p % 2, t, :], ident[:, :])
                    else:
                        wait_job(pe, ("turn", p, 0))
                        for t in range(2):
                            q = 2 * c + t
                            last = pe.matmul(J[:, t * C:(t + 1) * C], OT[:, q * P:(q + 1) * P], wo[:, p, :], start=True, stop=True)
                    last.then_inc(job_ready[i % 2], 1)

                def maxima(j, i):
                    par, h, t, (o, w) = j // 2 % 2, j % 2, i // NC, CHUNKS[i % NC]
                    rows = slice(0, DH) if h == 0 else slice(DH, P)
                    m = NT * NC * j + i
                    if m >= 2:
                        pe.wait_ge(mx_done, m - 1)
                    pe.matmul(MB[m % 2][:, 0:w], QA[rows, par, h, t * P:(t + 1) * P], KA[rows, par, h, o:o + w],
                              start=True, stop=True).then_inc(mx_ready, 1)

                def maxima_inputs(j):
                    p = j // 2
                    wait_job(pe, ("q", p, 0))
                    wait_job(pe, ("k", p, NC - 2))
                    wait_job(pe, ("k", p, NC - 1))

                pe.wait_ge(w_in, 16 * 6)
                pe.wait_ge(c_in, 32)
                for x in before():
                    job(x)
                maxima_inputs(0)
                for i in range(NT * NC):
                    maxima(0, i)
                job(("row", 0, 0))
                for j in range(heads):
                    p, par, h = j // 2, j // 2 % 2, j % 2
                    for t in range(KT + 1):
                        if t < KT:
                            n, r = KT * j + t, rows_of(t)
                            if t == 0:
                                wait_job(pe, ("row", j, 0))
                                pe.wait_ge(q_twice, 32 * (p + 1))
                                pe.wait_ge(k_twice, 32 * (p + 1))
                            if n >= 2:
                                pe.wait_ge(probs, n - 1)
                            pe.matmul(SB[n % 2][0:r, :], KA[:, par, h, t * P:t * P + r], QA[:, par, h, :], start=True, stop=False)
                            pe.matmul(SB[n % 2][0:r, :], KB[:, par, h, t * P:t * P + r], QB[:, par, h, :],
                                      start=False, stop=True).then_inc(sc_ready, 1)
                        if t == 1 and j + 1 < heads and h == 1:
                            maxima_inputs(j + 1)
                        for i in chunks_at(j, t):
                            maxima(j + 1, i)
                        for x in at(j, t):
                            job(x)
                        if t >= 1:
                            s, n = t - 1, KT * j + t - 1
                            r = rows_of(s)
                            pe.wait_ge(probs, n + 1)
                            if j >= 2 and s == 0:
                                pe.wait_ge(o_done, j - 1)
                            if s % NT == 0:
                                wait_job(pe, ("v", p, s // NT))
                            for q in range(NT):
                                last = pe.matmul(OB[j % 2][:, q * (DH + 1):(q + 1) * (DH + 1)], PR[0:r, n % 4, q * P:(q + 1) * P],
                                                 V[0:r, par, s, h, :], start=(s == 0 and q == 0), stop=(s == KT - 1),
                                                 skip_group_check=True)
                            last.then_inc(used, 1)
                for x in after:
                    job(x)

            @block.scalar
            def _(act):
                def job(x):
                    kind, p, c = x
                    i, par = place[x], p % 2
                    J = JB[i % 2]
                    if kind == "out":
                        return
                    act.wait_ge(job_ready[i % 2], i // 2 + 1)
                    if kind == "k":
                        o, w = CHUNKS[c]
                        if c == 0 and p >= 2:
                            act.wait_ge(sc_ready, 2 * KT * (p - 1))
                        act.activation(KA[0:DH, par, 0, o:o + w], J[0:DH, 0:w], ACT.Copy)
                        act.activation(KA[DH:P, par, 1, o:o + w], J[DH:P, 0:w], ACT.Copy).then_inc(k_high, 1)
                    elif kind == "q":
                        act.activation(QA[0:DH, par, 0, :], J[0:DH, :], ACT.Copy, scale=qscale[0:DH])
                        act.activation(QA[DH:P, par, 1, :], J[DH:P, :], ACT.Copy, scale=qscale[DH:P]).then_inc(q_high, 1)
                    elif kind == "v":
                        t0, n = VG[c]
                        if p >= 2:
                            act.wait_ge(used, 2 * KT * (p - 1))
                        r = rows_of(t0)
                        act.activation(V[0:r, par, t0:t0 + n, :, 0:DH].rearrange("p t h d -> p (t h) d"),
                                       J[0:r, 0:n * P].rearrange("p (th d) -> p th d", d=DH), ACT.Copy).then_inc(job_done[i % 2], 1)
                    elif kind == "row":
                        act.activation(QB[DH:DH + 1, p // 2 % 2, p % 2, :], J[0:1, :], ACT.Copy, scale=-1.0)\
                           .then_inc(job_done[i % 2], 1)
                    else:
                        if p >= 1:
                            wait_job(act, ("out", p - 1, 0))
                            wait_job(act, ("out", p - 1, 1))
                        act.activation(OT[:, 0:S], J[:, :], ACT.Copy).then_inc(job_done[i % 2], 1)

                act.wait_ge(prep, 1)
                for x in before():
                    job(x)
                job(("row", 0, 0))
                for j in range(heads):
                    for t in range(KT + 1):
                        if t < KT:
                            n, r = KT * j + t, rows_of(t)
                            if n >= 4:
                                act.wait_ge(used, n - 3)
                            act.wait_ge(sc_ready, n + 1)
                            act.activation(PR[0:r, n % 4, :], SB[n % 2][0:r, :], ACT.Exp,
                                           bias=keybias[0:r, t:t + 1] if masked else 0.0).then_inc(probs, 1)
                        for x in at(j, t):
                            job(x)
                for x in after:
                    job(x)

            @block.vector
            def _(dve):
                steps = [0]

                def link(ins):
                    steps[0] += 1
                    ins.then_inc(o_step, 1)
                    dve.wait_ge(o_step, steps[0])

                def job(x):
                    kind, p, c = x
                    i, par = place[x], p % 2
                    J = JB[i % 2]
                    if kind == "k":
                        o, w = CHUNKS[c]
                        dve.wait_ge(k_high, NC * p + c + 1)
                        dve.tensor_tensor(KB[0:DH, par, 0, o:o + w], J[0:DH, 0:w], KA[0:DH, par, 0, o:o + w], ALU.subtract)
                        dve.tensor_tensor(KB[0:DH, par, 1, o:o + w], J[DH:P, 0:w], KA[DH:P, par, 1, o:o + w],
                                          ALU.subtract).then_inc(job_done[i % 2], 1)
                    elif kind == "q":
                        dve.wait_ge(q_high, p + 1)
                        dve.scalar_tensor_tensor(QA[DH:P, par, 0, :], J[0:DH, :], qscale[0:DH], QA[0:DH, par, 0, :],
                                                 ALU.mult, ALU.subtract)
                        dve.scalar_tensor_tensor(QA[0:DH, par, 1, :], J[DH:P, :], qscale[DH:P], QA[DH:P, par, 1, :],
                                                 ALU.mult, ALU.subtract).then_inc(job_done[i % 2], 1)
                    elif kind == "out":
                        dve.wait_ge(job_ready[i % 2], i // 2 + 1)
                        dve.wait_ge(x_based, NT)
                        x2 = X[:, b * NT + 2 * c:b * NT + 2 * c + 2, :]
                        dve.tensor_tensor(x2, J[:, :].rearrange("p (t n) -> p t n", t=2), x2, ALU.add)\
                           .then_inc(job_done[i % 2], 1)

                def maxima(j, i):
                    o, w = CHUNKS[i % NC]
                    w = min(w, S2 - o)
                    m = NT * NC * j + i
                    out = mx[:, j % 2, i // NC, i % NC:i % NC + 1]
                    dve.wait_ge(mx_ready, m + 1)
                    if masked:
                        dve.tensor_tensor_reduce(MB[m % 2][:, 0:w], MB[m % 2][:, 0:w], maskadd[:, o:o + w], 1.0, -BIG,
                                                 ALU.add, ALU.max, out).then_inc(mx_done, 1)
                    else:
                        dve.tensor_reduce(out, MB[m % 2][:, 0:w], AX.X, ALU.max).then_inc(mx_done, 1)

                def maxima_end(j):
                    dve.wait_ge(mx_done, NT * NC * (j + 1))
                    if j >= 2:
                        dve.wait_ge(job_ready[place[("row", j - 2, 0)] % 2], place[("row", j - 2, 0)] // 2 + 1)
                    dve.tensor_reduce(m4[:, j % 2, :], mx[:, j % 2, :, :], AX.X, ALU.max).then_inc(m_ready, 1)

                def normalise(j):
                    p, h = j // 2, j % 2
                    o = OB[j % 2][:, 0:NT * (DH + 1)].rearrange("p (t d) -> p t d", t=NT)
                    dve.wait_ge(used, KT * (j + 1))
                    link(dve.reciprocal(rec[:, j % 2, :], o[:, :, DH]))
                    if p >= 2:
                        wait_job(dve, ("turn", p - 2, 0))
                    dve.tensor_tensor(On[:, p % 2, :, h * DH:(h + 1) * DH], o[:, :, 0:DH],
                                      rec[:, j % 2, :].unsqueeze(2).to_broadcast([P, NT, DH]), ALU.mult).then_inc(o_done, 1)

                if masked:
                    allowed = self.small[:, 1:2]
                    dve.wait_ge(m_in, 32)
                    link(dve.tensor_copy(maskadd, mask_rows))
                    link(dve.tensor_reduce(allowed, maskadd, AX.X, ALU.max))
                    link(dve.tensor_copy(keybias, mask_cols))
                    link(dve.tensor_scalar(maskadd, maskadd, -1.0, BIG, ALU.add, ALU.mult))
                    link(dve.tensor_scalar(maskadd, maskadd, allowed, None, ALU.mult))
                    link(dve.tensor_scalar(keybias, keybias, -1.0, BIG, ALU.add, ALU.mult))
                    link(dve.tensor_scalar(keybias, keybias, allowed, None, ALU.mult))
                    dve.tensor_scalar(qscale, allowed, DH ** -0.5, None, ALU.mult).then_inc(prep, 1)
                else:
                    dve.memset(qscale, DH ** -0.5).then_inc(prep, 1)
                dve.wait_ge(prep, 1)
                for x in before():
                    job(x)
                for i in range(NT * NC):
                    maxima(0, i)
                maxima_end(0)
                for j in range(heads):
                    for t in range(KT + 1):
                        if t == 1 and j >= 1:
                            normalise(j - 1)
                        for i in chunks_at(j, t):
                            maxima(j + 1, i)
                        for x in at(j, t):
                            job(x)
                        if t == 9 and j + 1 < heads:
                            maxima_end(j + 1)
                normalise(heads - 1)
                for x in after:
                    job(x)

    def top2(self, dve, link, logits, gates, exp_in, exp_out, to_exp, from_exp):
        rows, G = logits.shape[0], logits.shape[1]
        scratch = self.HTs[0:rows]
        n = G * E1 * E1
        more = scratch[:, 0:n].rearrange("p (g e j) -> p g e j", g=G, e=E1)
        same = scratch[:, n:2 * n].rearrange("p (g e j) -> p g e j", g=G, e=E1)
        rank = scratch[:, 2 * n:2 * n + G * E1].rearrange("p (g e) -> p g e", g=G)
        best = scratch[:, 2 * n + G * E1:2 * n + G * E1 + G]
        full = [rows, G, E1, E1]
        other = logits.unsqueeze(2).to_broadcast(full)
        own = logits.unsqueeze(3).to_broadcast(full)
        link(dve.tensor_tensor(more, other, own, ALU.is_gt))
        link(dve.tensor_tensor(same, other, own, ALU.is_equal))
        link(dve.tensor_tensor(same, same, self.tri[0:rows].unsqueeze(1).to_broadcast(full), ALU.mult))
        link(dve.tensor_tensor(more, more, same, ALU.add))
        link(dve.tensor_reduce(rank, more, AX.X, ALU.add))
        link(dve.tensor_scalar(rank, rank, 1.5, None, ALU.is_lt))
        link(dve.tensor_reduce(best, logits, AX.X, ALU.max))
        dve.tensor_tensor(exp_in, logits, best.unsqueeze(2).to_broadcast([rows, G, E1]), ALU.subtract).then_inc(to_exp, 1)
        dve.wait_ge(from_exp, 1)
        link(dve.tensor_tensor(gates, exp_out, rank, ALU.mult))
        link(dve.tensor_reduce(best, gates, AX.X, ALU.add))
        link(dve.reciprocal(best, best))
        link(dve.tensor_tensor(gates, gates, best.unsqueeze(2).to_broadcast([rows, G, E1]), ALU.mult))

    def mixture0(self, b):
        nc, a, HT, Hn, X, bank, W = self.nc, self.a, self.HT, self.Hn, self.X, self.bank, self.W
        KR = E0 * R0 // P
        wa = W[:, 0:KR * C].rearrange("p (k n) -> p k n", k=KR)
        wb = W[:, KR * C:2 * KR * C].rearrange("p (k n) -> p k n", k=KR)
        wr = W[:, 2048:2048 + CK * E0].rearrange("p (k n) -> p k n", k=CK)
        WB = W[:, 2560:2560 + CK * C].rearrange("p (k n) -> p k n", k=CK)
        logits = self.small[0:1, 32:40].rearrange("p (g e) -> p g e", g=1)
        gates = self.small[0:1, 40:48].rearrange("p (g e) -> p g e", g=1)
        exps = self.small[0:1, 48:64].rearrange("p (r g e) -> p r g e", r=2, g=1)
        gvec = self.small[:, 64:64 + KR]
        with self.stage() as (sem, ctx):
            w_in, lg_ready, to_exp, from_exp, step, g_ready, g_spread, b_scaled, wb_ready, wb_done, y_ready, based = (
                sem("e_w"), sem("e_lg"), sem("e_toexp"), sem("e_fromexp"), sem("e_step"), sem("e_gready"),
                sem("e_gspread"), sem("e_bscaled"), sem("e_wbready"), sem("e_wbdone"), sem("e_y"), sem("e_based"))
            block = ctx.enter_context(nc.Block())

            @block.sync
            def _(sp):
                sp.dma_start(wr, a["wr0T"].rearrange("(k p) e -> p k e", p=P)).then_inc(w_in, 16)
                sp.dma_start(wa, a["A0"].rearrange("(k p) n -> p k n", p=P)).then_inc(w_in, 16)
                sp.dma_start(wb, a["B0T"].rearrange("(k p) n -> p k n", p=P)).then_inc(w_in, 16)

            @block.gpsimd
            def _(pool):
                for t in range(NT):
                    x = X[:, b * NT + t, :]
                    pool.tensor_tensor(x, x, Hn[:, t, :], ALU.add).then_inc(based, 1)

            @block.tensor
            def _(pe):
                pe.wait_ge(w_in, 48)
                for k in range(CK):
                    last = pe.matmul(bank[0][0:1, 0:E0], HT[:, k, 0:1], wr[:, k, :], start=(k == 0), stop=(k == CK - 1))
                last.then_inc(lg_ready, 1)
                pe.wait_ge(g_ready, 1)
                pe.matmul(bank[1][:, 0:E0], self.ones[0:1, :], gates[0:1, 0, :], start=True, stop=True).then_inc(g_spread, 1)
                pe.wait_ge(b_scaled, KR)
                for m in range(CK):
                    for k in range(KR):
                        last = pe.matmul(bank[2][:, m * C:(m + 1) * C], wa[:, k, m * P:(m + 1) * P], wb[:, k, :],
                                         start=(k == 0), stop=(k == KR - 1))
                last.then_inc(wb_ready, 1)
                pe.wait_ge(wb_done, 1)
                for t in range(NT):
                    for k in range(CK):
                        last = pe.matmul(bank[3 + t][:, 0:C], HT[:, k, t * P:(t + 1) * P], WB[:, k, :],
                                         start=(k == 0), stop=(k == CK - 1))
                    last.then_inc(y_ready, 1)

            @block.scalar
            def _(act):
                act.wait_ge(to_exp, 1)
                act.activation(exps[:, 1], exps[:, 0], ACT.Exp).then_inc(from_exp, 1)
                act.wait_ge(wb_ready, 1)
                act.activation(WB, bank[2][:, :].rearrange("p (k n) -> p k n", k=CK), ACT.Copy).then_inc(wb_done, 1)

            @block.vector
            def _(dve):
                steps = [0]

                def link(ins):
                    steps[0] += 1
                    ins.then_inc(step, 1)
                    dve.wait_ge(step, steps[0])

                dve.wait_ge(lg_ready, 1)
                link(dve.tensor_copy(logits[:, 0, :], bank[0][0:1, 0:E0]))
                self.top2(dve, link, logits, gates, exps[:, 0], exps[:, 1], to_exp, from_exp)
                dve.tensor_copy(gvec[0:1, 0:1], gates[0:1, 0, 0:1]).then_inc(g_ready, 1)
                dve.wait_ge(g_spread, 1)
                dve.wait_ge(g_ready, 1)
                dve.tensor_copy(gvec[0:R0], bank[1][0:R0, 0:E0:2]).then_inc(step, 1)
                dve.tensor_copy(gvec[R0:P], bank[1][R0:P, 1:E0:2]).then_inc(step, 1)
                steps[0] += 2
                dve.wait_ge(step, steps[0])
                dve.wait_ge(w_in, 48)
                for k in range(KR):
                    dve.tensor_scalar(wb[:, k, :], wb[:, k, :], gvec[:, k:k + 1], None, ALU.mult).then_inc(b_scaled, 1)
                dve.wait_ge(based, NT)
                for t in range(NT):
                    x = X[:, b * NT + t, :]
                    dve.wait_ge(y_ready, t + 1)
                    dve.tensor_tensor(x, bank[3 + t][:, 0:C], x, ALU.add).then_inc(step, 1)

    def attention1(self, b):
        nc, a, HT, bank, W = self.nc, self.a, self.HT, self.bank, self.W
        w = W[:, 0:CK * 3 * C].rearrange("p (k n) -> p k n", k=CK)
        bias = W[:, 1536:1536 + 3 * C]
        gamma = W[:, 2304:2304 + 3 * C]
        alpha = self.bias[:, 0:C]
        Kb = [W[:, 4096 + 1024 * i:5120 + 1024 * i] for i in range(B)]
        vflat = self.V[:, :, :, :, :].rearrange("p a k h d -> p (a k h d)")
        Vb = [vflat[:, 1024 * i:1024 * (i + 1)] for i in range(3)] + [self.C0[:, 0:1024]]
        q1 = self.On[:, :, :, :].rearrange("p a t n -> p (a t n)")
        prod = [self.PR[:, 2 * i:2 * i + 2, :].rearrange("p r n -> p (r n)") for i in range(2)]
        A = self.Hn[:, :, :].rearrange("p t n -> p (t n)")
        R = NT * H
        sc = self.small[:, 0:R * B].rearrange("p (r s) -> p r s", s=B)[:, :, 0:b + 1]
        pr = self.small[:, R * B:2 * R * B - R].rearrange("p (r s) -> p r s", s=B - 1)
        m = self.bias[:, 512:512 + R]
        full = [P, R, b + 1]
        with self.stage() as (sem, ctx):
            w_in, b_in, y_ready, step, to_exp, from_exp = (
                sem("t_w"), sem("t_b"), sem("t_y"), sem("t_step"), sem("t_toexp"), sem("t_fromexp"))
            block = ctx.enter_context(nc.Block())

            @block.sync
            def _(sp):
                sp.dma_start(w, a["w1_in"].rearrange("(k p) n -> p k n", p=P)).then_inc(w_in, 16)
                sp.dma_start(bias, a["b1_in"].partition_broadcast(P)).then_inc(b_in, 16)
                sp.dma_start(gamma, a["gamma1"].partition_broadcast(P)).then_inc(b_in, 16)
                sp.dma_start(alpha, a["alpha1"].partition_broadcast(P)).then_inc(b_in, 16)

            @block.tensor
            def _(pe):
                pe.wait_ge(w_in, 16)
                for t in range(NT):
                    for o, n, J in ((0, 2 * C, bank[2 * t]), (2 * C, C, bank[2 * t + 1])):
                        for k in range(CK):
                            last = pe.matmul(J[:, 0:n], HT[:, k, t * P:(t + 1) * P], w[:, k, o:o + n],
                                             start=(k == 0), stop=(k == CK - 1))
                    last.then_inc(y_ready, 1)

            @block.scalar
            def _(act):
                act.wait_ge(to_exp, 1)
                act.activation(sc, sc, ACT.Exp, scale=D ** -0.5).then_inc(from_exp, 1)

            @block.vector
            def _(dve):
                steps = [0]

                def done(ins):
                    steps[0] += 1
                    ins.then_inc(step, 1)

                def link(ins):
                    done(ins)
                    dve.wait_ge(step, steps[0])

                dve.wait_ge(b_in, 48)
                for t in range(NT):
                    dve.wait_ge(y_ready, t + 1)
                    parts = [(q1, bank[2 * t][:, 0:C], 0), (Kb[b], bank[2 * t][:, C:2 * C], C), (Vb[b], bank[2 * t + 1][:, 0:C], 2 * C)]
                    for dst, src, o in parts:
                        done(dve.tensor_tensor(dst[:, t * C:(t + 1) * C], src, bias[:, o:o + C], ALU.add))
                    dve.wait_ge(step, steps[0])
                    for dst, _, o in parts:
                        d = dst[:, t * C:(t + 1) * C]
                        done(dve.tensor_tensor(d, d, gamma[:, o:o + C], ALU.mult))
                dve.wait_ge(step, steps[0])
                for s in range(b + 1):
                    link(dve.tensor_tensor(prod[s % 2], q1, Kb[s], ALU.mult))
                    done(dve.tensor_reduce(sc[:, :, s:s + 1].rearrange("p r o -> p (r o)"),
                                           prod[s % 2].rearrange("p (r d) -> p r d", d=D), AX.X, ALU.add))
                dve.wait_ge(step, steps[0])
                link(dve.tensor_reduce(m, sc, AX.X, ALU.max))
                dve.tensor_tensor(sc, sc, m.unsqueeze(2).to_broadcast(full), ALU.subtract).then_inc(to_exp, 1)
                dve.wait_ge(from_exp, 1)
                link(dve.tensor_reduce(m, sc, AX.X, ALU.add))
                link(dve.reciprocal(m, m))
                link(dve.tensor_tensor(sc, sc, m.unsqueeze(2).to_broadcast(full), ALU.mult))
                for s in range(b + 1):
                    dst = A if s == 0 else prod[s % 2]
                    link(dve.tensor_tensor(dst.rearrange("p (r d) -> p r d", d=D), Vb[s].rearrange("p (r d) -> p r d", d=D),
                                           sc[:, :, s].unsqueeze(2).to_broadcast([P, R, D]), ALU.mult))
                    if s > 0:
                        link(dve.tensor_tensor(A, A, dst, ALU.add))
                done(dve.tensor_tensor(self.Hn[:, :, :], self.Hn[:, :, :], alpha.unsqueeze(1).to_broadcast([P, NT, C]), ALU.mult))

    def expert_products(self):
        nc, a, bank, W = self.nc, self.a, self.bank, self.W
        KF = F1 // P
        WE = W[:, 0:CK * E1 * C].rearrange("p (k e n) -> p k e n", k=CK, e=E1)
        vflat = self.V[:, :, :, :, :].rearrange("p a k h d -> p (a k h d)")
        pflat = self.PR[:, :, :].rearrange("p r n -> p (r n)")
        first = [W[:, 4096:6144], vflat[:, 0:2048]]
        second = [W[:, 6144:8192], pflat]
        first, second = ([x.rearrange("p (k n) -> p k n", k=KF) for x in y] for y in (first, second))
        with self.stage() as (sem, ctx):
            in0, in1, ready, taken = sem("w_in0"), sem("w_in1"), sem("w_ready"), sem("w_taken")
            block = ctx.enter_context(nc.Block())

            @block.sync
            def _(sp):
                for e in range(E1):
                    if e >= 2:
                        sp.wait_ge(ready, e - 1)
                    sp.dma_start(first[e % 2], a["w_in1"][e].rearrange("(k p) n -> p k n", p=P)).then_inc((in0, in1)[e % 2], 16)
                    sp.dma_start(second[e % 2], a["w_out1T"][e].rearrange("(k p) n -> p k n", p=P)).then_inc((in0, in1)[e % 2], 16)

            @block.tensor
            def _(pe):
                for e in range(E1):
                    pe.wait_ge((in0, in1)[e % 2], 32 * (e // 2 + 1))
                    if e >= 2:
                        pe.wait_ge(taken, e - 1)
                    for m in range(CK):
                        for k in range(KF):
                            last = pe.matmul(bank[e % 2][:, m * C:(m + 1) * C], first[e % 2][:, k, m * P:(m + 1) * P],
                                             second[e % 2][:, k, :], start=(k == 0), stop=(k == KF - 1))
                    last.then_inc(ready, 1)

            @block.scalar
            def _(act):
                for e in range(E1):
                    act.wait_ge(ready, e + 1)
                    act.activation(WE[:, :, e, :], bank[e % 2][:, :].rearrange("p (k n) -> p k n", k=CK), ACT.Copy).then_inc(taken, 1)

    def mixture1(self, b):
        nc, a, HT, X, bank, W = self.nc, self.a, self.HT, self.X, self.bank, self.W
        WE = W[:, 0:CK * E1 * C].rearrange("p (k n) -> p k n", k=CK)
        wg = self.bias[:, 0:CK * E1].rearrange("p (k n) -> p k n", k=CK)
        G = NT * E1
        logits, gates, ein, eout = (self.small[:, G * i:G * (i + 1)].rearrange("p (g e) -> p g e", g=NT) for i in range(4))
        YB = bank[2:6]
        with self.stage() as (sem, ctx):
            w_in, lg_ready, to_exp, from_exp, step, y_ready, y_done = (
                sem("g_w"), sem("g_lg"), sem("g_toexp"), sem("g_fromexp"), sem("g_step"), sem("g_y"), sem("g_ydone"))
            block = ctx.enter_context(nc.Block())

            @block.sync
            def _(sp):
                sp.dma_start(wg, a["wg1T"].rearrange("(k p) e -> p k e", p=P)).then_inc(w_in, 16)

            @block.tensor
            def _(pe):
                pe.wait_ge(w_in, 16)
                for t in range(NT):
                    for k in range(CK):
                        last = pe.matmul(bank[0][:, t * E1:(t + 1) * E1], HT[:, k, t * P:(t + 1) * P], wg[:, k, :],
                                         start=(k == 0), stop=(k == CK - 1))
                last.then_inc(lg_ready, 1)
                for n in range(NT * E1 // 2):
                    t, e2 = n % NT, n // NT
                    if n >= 4:
                        pe.wait_ge(y_done, 2 * (n - 3))
                    for k in range(CK):
                        last = pe.matmul(YB[n % 4][:, :], HT[:, k, t * P:(t + 1) * P], WE[:, k, 2 * C * e2:2 * C * (e2 + 1)],
                                         start=(k == 0), stop=(k == CK - 1))
                    last.then_inc(y_ready, 1)

            @block.scalar
            def _(act):
                act.wait_ge(to_exp, 1)
                act.activation(eout, ein, ACT.Exp).then_inc(from_exp, 1)

            @block.vector
            def _(dve):
                steps = [0]

                def link(ins):
                    steps[0] += 1
                    ins.then_inc(step, 1)
                    dve.wait_ge(step, steps[0])

                dve.wait_ge(lg_ready, 1)
                link(dve.tensor_copy(logits, bank[0][:, 0:G].rearrange("p (g e) -> p g e", g=NT)))
                self.top2(dve, link, logits, gates, ein, eout, to_exp, from_exp)
                n = 0
                for e2 in range(E1 // 2):
                    for t in range(NT):
                        x = X[:, b * NT + t, :]
                        for h in range(2):
                            e = 2 * e2 + h
                            if h == 0:
                                dve.wait_ge(y_ready, n // 2 + 1)
                                if n >= 2 * NT:
                                    dve.wait_ge(y_done, n - 2 * NT + 2)
                            else:
                                dve.wait_ge(y_done, n)
                            dve.scalar_tensor_tensor(x, YB[n // 2 % 4][:, h * C:(h + 1) * C], gates[:, t, e:e + 1], x,
                                                     ALU.mult, ALU.add).then_inc(y_done, 1)
                            n += 1

    def run(self):
        self.load_inputs()
        self.cross_constants()
        for b in range(B):
            self.norm(b)
            self.self_project(b)
            self.self_attend(b)
            self.project_out(b, self.a["w0_out"], self.a["b0_out"])
            self.norm(b)
            self.cross_attention(b, 8, ("xq0", "xk0", "xv0", "xo0", "xb0"), True)
            self.norm(b)
            self.mixture0(b)
        for b in range(B):
            self.norm(b)
            self.attention1(b)
            self.project_out(b, self.a["w1_out"], self.a["b1_out"], self.a["gamma2"])
        self.cross_constants()
        for b in range(B):
            self.norm(b)
            self.cross_attention(b, 16, ("xq1", "xk1", "xv1", "xo1", "xb1"), False)
        self.expert_products()
        for b in range(B):
            self.norm(b)
            self.mixture1(b)
        self.store_outputs()


def layouts(i):
    import numpy as np
    g = {k: np.asarray(v) for k, v in i.items()}

    def flat(name):
        return g[name].reshape(-1)

    mask = g["mask_BxS2_bk0"]
    padded = np.zeros((B, KT * P), mask.dtype)
    padded[:, :S2] = mask
    out = {
        "x": g["x"], "ctxT": g["ctx_768"].transpose(0, 2, 1),
        "mask": mask, "maskT": padded.reshape(B, KT, P).transpose(0, 2, 1),
        "w0_in": g["L0_attn_in_proj_weight"].T, "b0_in": g["L0_attn_in_proj_bias"],
        "b0_cols": g["L0_attn_in_proj_bias"][0:2 * C].reshape(4, P).T,
        "w0_out": g["L0_attn_out_proj_weight"].T, "b0_out": g["L0_attn_out_proj_bias"],
        "xq0": g["L0_xattn_W_q"], "xk0": g["L0_xattn_W_k"], "xv0": g["L0_xattn_W_v"], "xo0": g["L0_xattn_W_o"],
        "xb0": g["L0_xattn_b_o"],
        "wr0T": g["L0_ffn_Wr"].T, "A0": g["L0_ffn_A"].reshape(E0 * R0, C),
        "B0T": g["L0_ffn_Bw"].transpose(0, 2, 1).reshape(E0 * R0, C),
        "w1_in": g["L1_attn_in_proj_weight"].T, "b1_in": g["L1_attn_in_proj_bias"],
        "gamma1": flat("L1_attn_gamma"), "alpha1": flat("L1_attn_linear_alpha"), "gamma2": flat("L1_attn_linear_gamma"),
        "w1_out": g["L1_attn_out_proj_weight"].T, "b1_out": g["L1_attn_out_proj_bias"],
        "xq1": g["L1_xattn_Wq"], "xk1": g["L1_xattn_Wk"], "xv1": g["L1_xattn_Wv"], "xo1": g["L1_xattn_Wo"],
        "xb1": g["L1_xattn_bo"],
        "wg1T": g["L1_ffn_w_gate"].T, "w_in1": g["L1_ffn_w_in"], "w_out1T": g["L1_ffn_w_out"].transpose(0, 2, 1),
    }
    return {k: np.ascontiguousarray(v) for k, v in out.items()}


def kernel(**inputs):
    import concourse.bacc as _bacc
    from concourse.bass_utils import run_bass_kernel_spmd as _run

    nc = _bacc.Bacc("TRN2", target_bir_lowering=False, num_devices=1)
    arrays = layouts(inputs)
    aps = {k: nc.dram_tensor(f"in_{k}", v.shape, mybir.dt.from_np(v.dtype), kind="ExternalInput").ap()
           for k, v in arrays.items()}
    out = nc.dram_tensor("out_x", (B, S, C), F32, kind="ExternalOutput").ap()
    with ExitStack() as ctx:
        Core(nc, ctx, aps, out).run()
    r = _run(nc, [{f"in_{k}": v for k, v in arrays.items()}], core_ids=[0])
    return r.results[0]["out_x"]
```

```python
from contextlib import ExitStack, contextmanager

import concourse.bass as bass
from concourse import mybir

F32 = mybir.dt.float32
F32R = mybir.dt.float32r
U8 = mybir.dt.uint8
ALU = mybir.AluOpType
ACT = mybir.ActivationFunctionType
AX = mybir.AxisListType

P = 128
B, S, C = 4, 512, 256
NT = S // P
CK = C // P
H, D = 16, 16
S2, CC = 1601, 192
S2E = S2 + S2 % 2
KT = -(-S2 // P)
TAIL = S2 - (KT - 1) * P
DH = 64
E0, R0 = 8, 64
E1, F1 = 8, 1024
EPS = 1e-5
BIG = 3e38
CHUNKS = [(0, 400), (400, 400), (800, 400), (1200, S2E - 1200)]
NC = len(CHUNKS)
VG = [(0, 4), (4, 4), (8, 4), (12, KT - 12)]


def rows_of(kt):
    return P if kt < KT - 1 else TAIL


def raw(ap):
    return ap.bitcast(F32)


class Core:

    def __init__(self, nc, ctx, a, out):
        self.nc, self.a, self.out, self.stages = nc, a, out, 0

        self.x_out = ctx.enter_context(nc.semaphore("x_out"))
        self.ctx_in, self.xk_in, self.xq_in, self.xv_in, self.mask_in = (
            ctx.enter_context(nc.semaphore(n)) for n in ("ctx_in", "xk_in", "xq_in", "xv_in", "mask_in"))
        self.ctx_loads = self.weight_loads = self.mask_loads = 0

        def sb(name, shape, dt=F32):
            return ctx.enter_context(nc.sbuf_tensor(name, shape, dt))

        self.X = sb("X", [P, B * NT, C])
        self.Hn = sb("Hn", [P, NT, C])
        self.HT = sb("HT", [P, CK, S])
        self.ident = sb("ident", [P, P])
        self.stats = sb("stats", [P, NT, 6])
        self.mv = sb("mv", [P, NT, 2])
        self.std = sb("std", [P, NT])
        self.rstd = sb("rstd", [P, NT])
        self.KA = sb("KA", [P, 2, 2, S2E], F32R)
        self.KB = sb("KB", [DH + 1, 2, 2, S2E], F32R)
        self.QA = sb("QA", [P, 2, 2, S], F32R)
        self.QB = sb("QB", [DH + 1, 2, 2, S], F32R)
        self.V = sb("V", [P, 2, KT, 2, DH])
        self.SV = self.V[:, :, :, :, :].rearrange("p a k h d -> p (a k h d)")[:, 0:NT * H * 32].rearrange(
            "p (t h d) -> p t h d", t=NT, h=H)
        self.PR = sb("PR", [P, 6, S])
        self.ACC = sb("ACC", [P, 2, 2, S])
        self.On = self.ACC[:, :, 0, :].rearrange("p a (t n) -> p a t n", t=NT)
        self.OT = sb("OT", [P, 1024])
        self.C0 = sb("C0", [P, S2E])
        self.C1 = sb("C1", [CC - P, S2E])
        self.W = sb("W", [P, 8192])
        self.HI = self.KA[:, :, :, :].rearrange("p a h n -> p (a h n)")[:, 8 * S:12 * S].rearrange("p (i n) -> p i n", i=4)
        self.LO = sb("LO", [P, 4, S], F32R)
        self.SK1 = sb("SK1", [P, 8 * S], F32R)
        self.bias = sb("bias", [P, 3 * C])
        self.mx = sb("mx", [P, 2, NT, NC])
        self.m4 = sb("m4", [P, 2, NT])
        self.rec = sb("rec", [P, 2, NT])
        self.small = sb("small", [P, 512])
        self.tri = sb("tri", [P, E1, E1])
        self.ones = sb("ones", [P, P])
        self.HTs = self.OT
        self.bank = [ctx.enter_context(nc.psum_tensor(f"bank{i}", [P, 512], F32)) for i in range(8)]

    @contextmanager
    def stage(self):
        nc, names = self.nc, []
        self.stages += 1

        def sem(name):
            names.append(nc.alloc_semaphore(f"{name}_{self.stages}"))
            return names[-1]

        with ExitStack() as ctx:
            yield sem, ctx
        nc.clear_and_free_semaphores(names)
        nc.all_engine_barrier()

    def cross_weights(self, heads):
        W, inner = self.W, heads * DH
        return (W[:, 0:CK * inner].rearrange("p (k n) -> p k n", k=CK),
                W[:, 2 * inner:4 * inner].rearrange("p (k n) -> p k n", k=2),
                W[:, 4 * inner:6 * inner].rearrange("p (k n) -> p k n", k=2),
                W[:, 6 * inner:8 * inner].rearrange("p (j n) -> p j n", j=heads // 2))

    def masks(self):
        W = self.W
        return W[:, 6000:6000 + (S2 + 3) // 4 + 1].bitcast(U8)[:, 0:S2], W[:, 6500:6504].bitcast(U8)[:, 0:KT]

    def load_context(self, sp, b):
        a = self.a
        self.ctx_loads += 1
        sp.dma_start(self.C0[:, 0:S2], a["ctxT"][b, 0:P, :]).then_inc(self.ctx_in, 16)
        sp.dma_start(self.C1[:, 0:S2], a["ctxT"][b, P:CC, :]).then_inc(self.ctx_in, 16)

    def load_cross_weights(self, sp, heads, names):
        a = self.a
        wq, wk, wv, wo = self.cross_weights(heads)
        self.weight_loads += 1
        sp.dma_start(wk[:, 0, :], a[names[1]][0:P, :]).then_inc(self.xk_in, 16)
        sp.dma_start(wk[0:CC - P, 1, :], a[names[1]][P:CC, :]).then_inc(self.xk_in, 16)
        sp.dma_start(wq, a[names[0]].rearrange("(k p) n -> p k n", p=P)).then_inc(self.xq_in, 16)
        sp.dma_start(wv[:, 0, :], a[names[2]][0:P, :]).then_inc(self.xv_in, 16)
        sp.dma_start(wv[0:CC - P, 1, :], a[names[2]][P:CC, :]).then_inc(self.xv_in, 16)
        sp.dma_start(wo, a[names[3]].rearrange("(j p) n -> p j n", p=P)).then_inc(self.xv_in, 16)

    def load_masks(self, sp, b):
        rows, cols = self.masks()
        self.mask_loads += 1
        sp.dma_start(rows, self.a["mask"][b].partition_broadcast(P)).then_inc(self.mask_in, 16)
        sp.dma_start(cols, self.a["maskT"][b]).then_inc(self.mask_in, 16)

    def load_inputs(self):
        nc, a = self.nc, self.a
        with self.stage() as (sem, ctx):
            x_in, zeroed, made = sem("x_in"), sem("zeroed"), sem("made")
            block = ctx.enter_context(nc.Block())

            @block.sync
            def _(sp):
                sp.dma_start(self.X[:, :, :], a["x"].rearrange("b (t p) c -> p (b t) c", p=P)).then_inc(x_in, 16)
                sp.wait_ge(x_in, 16)

            @block.gpsimd
            def _(pool):
                pool.memset(self.ident[:, :], 0.0).then_inc(zeroed, 1)
                pool.wait_ge(zeroed, 1)
                pool.affine_select(out=self.ident[:, :], in_=self.ident[:, :], compare_op=ALU.not_equal, fill=1.0,
                                   base=0, pattern=[[-1, P]], channel_multiplier=1).then_inc(made, 1)
                pool.memset(self.ones[:, :], 1.0).then_inc(made, 1)
                pool.memset(self.tri[:, :, :], 1.0).then_inc(zeroed, 1)
                pool.wait_ge(zeroed, 2)
                pool.affine_select(out=self.tri[:, :, :], in_=self.tri[:, :, :], compare_op=ALU.is_gt, fill=0.0,
                                   base=0, pattern=[[1, E1], [-1, E1]], channel_multiplier=0).then_inc(made, 1)
                pool.memset(self.C0[:, S2:S2E], 0.0).then_inc(made, 1)
                pool.memset(self.C1[:, S2:S2E], 0.0).then_inc(made, 1)

    def cross_constants(self):
        nc = self.nc
        with self.stage() as (sem, ctx):
            made = sem("ones_made")
            block = ctx.enter_context(nc.Block())

            @block.vector
            def _(dve):
                dve.memset(self.small[DH:DH + 1, :], 1.0).then_inc(made, 1)
                dve.wait_ge(made, 1)
                for par in range(2):
                    for a in range(2):
                        for o, w in CHUNKS:
                            dve.tensor_copy(self.KB[DH:DH + 1, par, a, o:o + w], self.small[DH:DH + 1, 0:w]).then_inc(made, 1)

    def store_outputs(self):
        nc = self.nc
        with ExitStack() as ctx:
            x_out = self.x_out
            block = ctx.enter_context(nc.Block())

            @block.sync
            def _(sp):
                sp.dma_start(self.out.rearrange("b (t p) c -> p (b t) c", p=P), self.X[:, :, :]).then_inc(x_out, 16)
                sp.wait_ge(x_out, 16)

    def norm(self, b):
        nc = self.nc
        X, Hn, HT = self.X, self.Hn, self.HT
        with self.stage() as (sem, ctx):
            step, var_ready, std_ready, rows_ready, turned = (
                sem("n_step"), sem("n_var"), sem("n_std"), sem("n_rows"), sem("n_turned"))
            block = ctx.enter_context(nc.Block())

            @block.vector
            def _(dve):
                for t in range(NT):
                    dve.bn_stats(self.stats[:, t, :], X[:, b * NT + t, :]).then_inc(step, 1)
                dve.wait_ge(step, NT)
                for t in range(NT):
                    dve.bn_aggr(self.mv[:, t, :], self.stats[:, t, :]).then_inc(step, 1)
                dve.wait_ge(step, 2 * NT)
                dve.tensor_scalar(self.std[:, :], self.mv[:, :, 1], EPS, None, ALU.add).then_inc(var_ready, 1)
                dve.wait_ge(std_ready, 1)
                dve.reciprocal(self.rstd[:, :], self.rstd[:, :]).then_inc(step, 1)
                dve.wait_ge(step, 2 * NT + 1)
                for t in range(NT):
                    dve.tensor_scalar(Hn[:, t, :], X[:, b * NT + t, :], self.mv[:, t, 0:1], self.rstd[:, t:t + 1],
                                      ALU.subtract, ALU.mult).then_inc(rows_ready, 1)
                dve.wait_ge(turned, 2)
                dve.tensor_copy(HT[:, 1, :], self.bank[1][:, :]).then_inc(step, 1)

            @block.scalar
            def _(act):
                act.wait_ge(var_ready, 1)
                act.activation(self.rstd[:, :], self.std[:, :], ACT.Sqrt).then_inc(std_ready, 1)
                act.wait_ge(turned, 1)
                act.activation(HT[:, 0, :], self.bank[0][:, :], ACT.Copy).then_inc(std_ready, 1)

            @block.tensor
            def _(pe):
                pe.wait_ge(rows_ready, NT)
                for k in range(CK):
                    for t in range(NT):
                        last = pe.transpose(self.bank[k][:, t * P:(t + 1) * P], Hn[:, t, k * P:(k + 1) * P], self.ident[:, :])
                    last.then_inc(turned, 1)

    def stacked(self, h, keys):
        if h < 8:
            t = self.KB if keys else self.KA
            flat = t[:, :, :, :].rearrange("p a h n -> p (a h n)")
            return flat[0:3 * D + 1, h * S:(h + 1) * S]
        if keys:
            return self.SK1[0:3 * D + 1, (h - 8) * S:(h - 7) * S]
        t = self.QA if h < 12 else self.QB
        return t[:, :, :, :].rearrange("p a h n -> p (a h n)")[0:3 * D + 1, (h % 4) * S:(h % 4 + 1) * S]

    def self_project(self, b):
        nc, a, HT, bank = self.nc, self.a, self.HT, self.bank
        w = self.W[:, 0:CK * 3 * C].rearrange("p (k n) -> p k n", k=CK)
        full = self.W[:, 2048:3072].rearrange("p (r n) -> p r n", r=2)
        bcol = self.W[:, 3072:3076]
        vbias = self.bias[:, 0:C]
        HI, LO = self.HI, self.LO
        with self.stage() as (sem, ctx):
            w_in, b_in, ones, q_ready, full_ready, hi_ready, lo_ready, v_done = (
                sem("sp_w"), sem("sp_b"), sem("sp_ones"), sem("sp_q"), sem("sp_full"), sem("sp_hi"), sem("sp_lo"),
                sem("sp_v"))
            block = ctx.enter_context(nc.Block())

            @block.sync
            def _(sp):
                sp.dma_start(w, a["w0_in"].rearrange("(k p) n -> p k n", p=P)).then_inc(w_in, 16)
                sp.dma_start(bcol, a["b0_cols"]).then_inc(b_in, 16)
                sp.dma_start(vbias, a["b0_in"][2 * C:3 * C].partition_broadcast(P)).then_inc(b_in, 16)

            @block.gpsimd
            def _(pool):
                pool.memset(self.SV[:, :, :, :].rearrange("p t h d -> p (t h d)"), 0.0).then_inc(ones, 1)
                pool.wait_ge(ones, 1)
                pool.memset(self.SV[:, :, :, D:D + 1].rearrange("p t h o -> p (t h) o"), 1.0).then_inc(ones, 1)
                pool.wait_ge(ones, 2)
                for h in range(H):
                    pool.memset(raw(self.stacked(h, True)[2 * D:2 * D + 1]), 1.0).then_inc(ones, 1)

            @block.tensor
            def _(pe):
                pe.wait_ge(w_in, 16)
                for i in range(4):
                    if i >= 2:
                        pe.wait_ge(full_ready, i - 1)
                    for k in range(CK):
                        last = pe.matmul(bank[i % 2][:, :], w[:, k, i * P:(i + 1) * P], HT[:, k, :],
                                         start=(k == 0), stop=(k == CK - 1))
                    last.then_inc(q_ready, 1)
                for t in range(NT):
                    for k in range(CK):
                        last = pe.matmul(bank[2 + t][:, 0:C], HT[:, k, t * P:(t + 1) * P], w[:, k, 2 * C:3 * C],
                                         start=(k == 0), stop=(k == CK - 1))
                    last.then_inc(q_ready, 1)

            @block.scalar
            def _(act):
                for i in range(4):
                    act.wait_ge(full_ready, i + 1)
                    act.activation(HI[:, i, :], full[:, i % 2, :], ACT.Copy).then_inc(hi_ready, 1)

            @block.vector
            def _(dve):
                dve.wait_ge(b_in, 32)
                for i in range(5):
                    if i < 4:
                        dve.wait_ge(q_ready, i + 1)
                        if i >= 2:
                            dve.wait_ge(lo_ready, i - 1)
                        dve.tensor_scalar(full[:, i % 2, :], bank[i % 2][:, :], bcol[:, i:i + 1],
                                          D ** -0.5 if i < 2 else 1.0, ALU.add, ALU.mult).then_inc(full_ready, 1)
                    if i >= 1:
                        dve.wait_ge(hi_ready, i)
                        dve.tensor_tensor(LO[:, i - 1, :], full[:, (i - 1) % 2, :], HI[:, i - 1, :],
                                          ALU.subtract).then_inc(lo_ready, 1)
                dve.wait_ge(ones, 2)
                for t in range(NT):
                    dve.wait_ge(q_ready, 5 + t)
                    dve.tensor_tensor(self.SV[:, t, :, 0:D], bank[2 + t][:, 0:C].rearrange("p (h d) -> p h d", h=H),
                                      vbias.rearrange("p (h d) -> p h d", h=H), ALU.add).then_inc(v_done, 1)

    def self_attend(self, b):
        nc, bank = self.nc, self.bank
        SPAN = S + (NT - 1) * P
        GH = 4
        GN = GH * NT
        SLOT = P // GH
        relq = self.C0[:, 0:SPAN]
        relk = self.OT[:, 0:SPAN]
        raised = self.C0[:, SPAN:SPAN + S]
        stripq = self.ACC[:, :, :, :].rearrange("p a h n -> p (a h n)")[:, 0:2 * SPAN].rearrange("p (r x) -> p r x", r=2)
        stripk = self.W[:, 0:2 * GH * SPAN].rearrange("p (r x) -> p r x", r=2 * GH)
        vflat = self.V[:, :, :, :, :].rearrange("p a k h d -> p (a k h d)")
        beside = NT * H * SLOT
        PR = [self.PR[:, i, :] for i in range(6)] + [vflat[:, beside + i * S:beside + (i + 1) * S] for i in range(2)]
        RING = len(PR)
        V, A, m4, ident = self.SV, self.Hn, self.m4, self.ident
        rec = self.small[:, 0:GN].rearrange("p (t h) -> p t h", t=NT)
        slopes = [2.0 ** (-(i + 1) / 2) for i in range(H)]
        HI, LO = self.HI, self.LO
        N = H * NT
        SB, MB, OB, RB = bank[0:3], bank[3:5], bank[5:7], bank[7]

        def tile_of(n):
            g, t, h = n // GN, n % GN // GH, n % GH
            return g, t, GH * g + h

        def row_at(n):
            k = (n + GN) // NT - 1
            return k if n % NT == 2 and k < H else None

        with self.stage() as (sem, ctx):
            rel, sq_ready, sk_ready, sc_ready, biased, probs, used, mx_ready, mx_done, row_ready, row_done = (
                sem("sa_rel"), sem("sa_sq"), sem("sa_sk"), sem("sa_scores"), sem("sa_biased"), sem("sa_probs"),
                sem("sa_used"), sem("sa_mxready"), sem("sa_mxdone"), sem("sa_rowready"), sem("sa_rowdone"))
            o_raised, o_turned, o_step, o_done = sem("sa_raised"), sem("sa_turned"), sem("sa_ostep"), sem("sa_odone")
            stacked = [sem(f"sa_stacked{h}") for h in range(H)]
            block = ctx.enter_context(nc.Block())

            @block.sync
            def _(sp):
                for h in range(H):
                    g, src = h // 8, slice(D * (h % 8), D * (h % 8 + 1))
                    for keys, parts in ((False, (HI, LO, HI)), (True, (HI, HI, LO))):
                        dst = self.stacked(h, keys)
                        for part, row in zip(parts, (0, D, 2 * D + 1)):
                            sp.dma_start(raw(dst[row:row + D]), raw(part[src, 2 * keys + g, :])).then_inc(stacked[h], 16)

            @block.gpsimd
            def _(pool):
                pool.iota(relq, [[-1, SPAN]], base=(NT - 1) * P, channel_multiplier=1,
                          allow_small_or_imprecise_dtypes=True).then_inc(rel, 1)
                pool.iota(relk, [[1, SPAN]], base=-(NT - 1) * P, channel_multiplier=-1,
                          allow_small_or_imprecise_dtypes=True).then_inc(rel, 1)

            @block.tensor
            def _(pe):
                def maxima(m):
                    h, t = m // NT, m % NT
                    if t == 0:
                        pe.wait_ge(stacked[h], 16 * 6)
                    if m >= 2:
                        pe.wait_ge(mx_done, m - 1)
                    pe.matmul(MB[m % 2][:, :], self.stacked(h, False)[0:2 * D, t * P:(t + 1) * P],
                              self.stacked(h, True)[0:2 * D, :], start=True, stop=True).then_inc(mx_ready, 1)

                def max_row(h):
                    pe.wait_ge(mx_done, NT * (h + 1))
                    if h >= 1:
                        pe.wait_ge(row_done, h)
                    for t in range(NT):
                        last = pe.matmul(RB[0:1, t * P:(t + 1) * P], m4[:, h % 2, t:t + 1], ident[:, :],
                                         start=True, stop=True)
                    last.then_inc(row_ready, 1)

                def values(q):
                    g, t = q // NT, q % NT
                    pe.wait_ge(probs, GH * (q + 1))
                    if t == 0 and g >= 2:
                        pe.wait_ge(o_done, g - 1)
                    for h in range(GH):
                        last = pe.matmul(OB[g % 2][h * SLOT:(h + 1) * SLOT, :], V[:, t, GH * g + h, :],
                                         PR[(GH * q + h) % RING], start=(t == 0), stop=(t == NT - 1),
                                         tile_position=(0, h * SLOT))
                    last.then_inc(used, 1)

                def turn(g):
                    pe.wait_ge(o_raised, g + 1)
                    for t in range(NT):
                        last = pe.transpose(OB[g % 2][:, t * P:(t + 1) * P], raised[:, t * P:(t + 1) * P], ident[:, :])
                    last.then_inc(o_turned, 1)

                for m in range(GN):
                    maxima(m)
                    if m >= NT + 2 and row_at(m - GN) is not None:
                        max_row(row_at(m - GN))
                for n in range(N):
                    g, t, h = tile_of(n)
                    if n >= 3:
                        pe.wait_ge(probs, n - 2)
                    if t == 0:
                        pe.wait_ge(row_done, h + 1)
                    pe.matmul(SB[n % 3][:, :], self.stacked(h, True)[:, t * P:(t + 1) * P], self.stacked(h, False),
                              start=True, stop=True).then_inc(sc_ready, 1)
                    if row_at(n) is not None:
                        max_row(row_at(n))
                    if n + GN < N:
                        maxima(n + GN)
                    if n % GH == GH - 1 and n >= GH:
                        values(n // GH - 1)
                    if n % GN == 6 and g >= 1:
                        turn(g - 1)
                values(N // GH - 1)
                turn(H // GH - 1)

            @block.scalar
            def _(act):
                def make_stripq(h):
                    if h >= 2:
                        act.wait_ge(mx_done, NT * (h - 1))
                    act.activation(stripq[:, h % 2, :], relq, ACT.Relu, bias=8.0, scale=-slopes[h]).then_inc(sq_ready, 1)

                def make_stripk(h):
                    if h >= 2 * GH:
                        act.wait_ge(biased, GN * (h // GH - 1))
                    act.activation(stripk[:, h % (2 * GH), :], relk, ACT.Relu, bias=8.0, scale=-slopes[h]).then_inc(sk_ready, 1)

                def copy_row(h):
                    act.wait_ge(row_ready, h + 1)
                    act.activation(self.stacked(h, False)[2 * D:2 * D + 1, :], RB[0:1, :], ACT.Copy,
                                   scale=-1.0).then_inc(row_done, 1)

                def raise_outputs(g):
                    act.wait_ge(used, NT * (g + 1))
                    if g >= 1:
                        act.wait_ge(o_turned, g)
                    act.activation(raised, OB[g % 2][:, :], ACT.Copy).then_inc(o_raised, 1)

                act.wait_ge(rel, 2)
                make_stripq(0)
                make_stripq(1)
                for k in range(3):
                    make_stripk(k)
                    make_stripq(k + 2)
                    copy_row(k)
                make_stripk(3)
                for n in range(N):
                    g, t, h = tile_of(n)
                    if n >= RING:
                        act.wait_ge(used, n // GH - 1)
                    act.wait_ge(biased, n + 1)
                    act.activation(PR[n % RING], SB[n % 3][:, :], ACT.Exp).then_inc(probs, 1)
                    if row_at(n) is not None:
                        copy_row(row_at(n))
                    if n % NT == 2 and (n + 18) // NT < H:
                        make_stripq((n + 18) // NT)
                    if n % NT == 1 and GH + n // NT < H:
                        make_stripk(GH + n // NT)
                    if n % GN == 4 and g >= 1:
                        raise_outputs(g - 1)
                raise_outputs(H // GH - 1)

            @block.vector
            def _(dve):
                def maxima(m):
                    h, t = m // NT, m % NT
                    dve.wait_ge(mx_ready, m + 1)
                    if t == 0:
                        dve.wait_ge(sq_ready, h + 1)
                        if h >= 2:
                            dve.wait_ge(row_ready, h - 1)
                    dve.tensor_tensor_reduce(MB[m % 2][:, :], MB[m % 2][:, :], stripq[:, h % 2, (NT - 1 - t) * P:(NT - 1 - t) * P + S],
                                             1.0, -BIG, ALU.subtract, ALU.max, m4[:, h % 2, t:t + 1]).then_inc(mx_done, 1)

                def normalise(g):
                    o = OB[g % 2][:, :].rearrange("p (t h d) -> p t h d", t=NT, h=GH)
                    dve.wait_ge(o_turned, g + 1)
                    if g >= 1:
                        dve.wait_ge(o_done, g)
                    dve.reciprocal(rec, o[:, :, :, D]).then_inc(o_step, 1)
                    dve.wait_ge(o_step, g + 1)
                    dve.tensor_tensor(A[:, :, GH * g * D:GH * (g + 1) * D].rearrange("p t (h d) -> p t h d", h=GH), o[:, :, :, 0:D],
                                      rec.unsqueeze(3).to_broadcast([P, NT, GH, D]), ALU.mult).then_inc(o_done, 1)

                for m in range(GN):
                    maxima(m)
                for n in range(N):
                    g, t, h = tile_of(n)
                    dve.wait_ge(sc_ready, n + 1)
                    if t == 0:
                        dve.wait_ge(sk_ready, h + 1)
                    dve.tensor_tensor(SB[n % 3][:, :], SB[n % 3][:, :], stripk[:, h % (2 * GH), (NT - 1 - t) * P:(NT - 1 - t) * P + S],
                                      ALU.subtract).then_inc(biased, 1)
                    if n + GN < N:
                        maxima(n + GN)
                    if n % GN == 8 and g >= 1:
                        normalise(g - 1)
                normalise(H // GH - 1)

    def project_out(self, b, w_dram, bias_dram, gamma_dram=None, ahead=None):
        nc, a, A, HT, X, bank = self.nc, self.a, self.Hn, self.HT, self.X, self.bank
        w = self.OT[:, 0:CK * C].rearrange("p (k n) -> p k n", k=CK)
        bias, gamma = self.bias[:, 0:C], self.bias[:, C:2 * C]
        out = self.ACC[:, 0, 0, :].rearrange("p (r n) -> p r n", r=2)
        with self.stage() as (sem, ctx):
            w_in, b_in, turned, copied, y_ready, step = (
                sem("po_w"), sem("po_b"), sem("po_turned"), sem("po_copied"), sem("po_y"), sem("po_step"))
            block = ctx.enter_context(nc.Block())

            @block.sync
            def _(sp):
                sp.dma_start(w, w_dram.rearrange("(k p) n -> p k n", p=P)).then_inc(w_in, 16)
                sp.dma_start(bias, bias_dram.partition_broadcast(P)).then_inc(b_in, 16)
                if gamma_dram is not None:
                    sp.dma_start(gamma, gamma_dram.partition_broadcast(P)).then_inc(b_in, 16)
                if ahead is not None:
                    batch, heads, names, masked = ahead
                    self.load_context(sp, batch)
                    if masked:
                        self.load_masks(sp, batch)
                    self.load_cross_weights(sp, heads, names)

            @block.tensor
            def _(pe):
                for k in range(CK):
                    for t in range(NT):
                        last = pe.transpose(bank[k][:, t * P:(t + 1) * P], A[:, t, k * P:(k + 1) * P], self.ident[:, :])
                    last.then_inc(turned, 1)
                pe.wait_ge(w_in, 16)
                pe.wait_ge(copied, CK)
                for t in range(NT):
                    for k in range(CK):
                        last = pe.matmul(bank[2 + t][:, 0:C], HT[:, k, t * P:(t + 1) * P], w[:, k, :],
                                         start=(k == 0), stop=(k == CK - 1))
                    last.then_inc(y_ready, 1)

            @block.scalar
            def _(act):
                for k in range(CK):
                    act.wait_ge(turned, k + 1)
                    act.activation(HT[:, k, :], bank[k][:, :], ACT.Copy).then_inc(copied, 1)

            @block.vector
            def _(dve):
                dve.wait_ge(b_in, 16 if gamma_dram is None else 32)
                n = 0
                for t in range(NT):
                    x = X[:, b * NT + t, :]
                    dve.wait_ge(y_ready, t + 1)
                    dve.tensor_tensor(out[:, t % 2, :], bank[2 + t][:, 0:C], bias, ALU.add).then_inc(step, 1)
                    n += 1
                    dve.wait_ge(step, n)
                    if gamma_dram is not None:
                        dve.tensor_tensor(out[:, t % 2, :], out[:, t % 2, :], gamma, ALU.mult).then_inc(step, 1)
                        n += 1
                        dve.wait_ge(step, n)
                    dve.tensor_tensor(x, out[:, t % 2, :], x, ALU.add).then_inc(step, 1)
                    n += 1

    def cross_attention(self, b, heads, names, masked, next_context=None):
        nc, a, bank = self.nc, self.a, self.bank
        X, HT, C0, C1 = self.X, self.HT, self.C0, self.C1
        KA, KB, QA, QB, V, PR, ACC = self.KA, self.KB, self.QA, self.QB, self.V, self.PR, self.ACC
        OT, RD = self.OT[:, 0:S], self.OT[:, S:2 * S]
        mx, m4, ident, ones = self.mx, self.m4, self.ident, self.ones
        inner, pairs = heads * DH, heads // 2
        W = self.W
        wq, wk, wv, wo = self.cross_weights(heads)
        qscale = self.small[:, 0:1]
        keybias = self.small[:, 16:16 + KT]
        maskadd = W[:, 4096:4096 + S2] if masked else None
        mask_rows, mask_cols = self.masks()
        ctx_loads, weight_loads, mask_loads = self.ctx_loads, self.weight_loads, self.mask_loads
        SB, OB, MB, JB = bank[0:3], bank[3], bank[4:6], bank[6:8]
        TP = 2 * KT
        RING = 6

        def before():
            return [("k", 0, c) for c in range(NC)] + [("q", 0, 0)] + [("v", 0, g) for g in range(len(VG))]

        def at(p, t):
            jobs = []
            if p >= 1 and t in (2, 3, 4):
                jobs.append([("sum", p - 1, 0), ("out", p - 1, 0), ("out", p - 1, 1)][t - 2])
            if p + 1 < pairs:
                if t < 2:
                    jobs += [("k", p + 1, 2 * t), ("k", p + 1, 2 * t + 1)]
                if t == 2:
                    jobs.append(("q", p + 1, 0))
                if 5 <= t < 5 + len(VG):
                    jobs.append(("v", p + 1, t - 5))
                if t in (9, 12):
                    jobs.append(("row", 2 * p + (2 if t == 9 else 3), 0))
            return jobs

        first = [("row", 0, 0), ("row", 1, 0)]
        after = [("sum", pairs - 1, 0), ("out", pairs - 1, 0), ("out", pairs - 1, 1)]
        order = before() + first + [x for p in range(pairs) for t in range(KT + 1) for x in at(p, t)] + after
        place = {x: i for i, x in enumerate(order)}

        def chunks_at(p, t):
            if p + 1 == pairs or not 3 <= t <= 10:
                return []
            return [(2 * p + 2 + i // (NT * NC), i % (NT * NC)) for i in range(4 * (t - 3), 4 * (t - 2))]

        def sums_done(n):
            p, t, h = n // TP, n % TP // 2, n % 2
            return 2 * (KT - 1) * p + 2 * (max(t, 1) - 1) + h + 1

        with self.stage() as (sem, ctx):
            bo_in, prep, x_based = sem("x_boin"), sem("x_prep"), sem("x_based")
            sc_ready, probs, used, o_step, o_done, summed, normed = (
                sem("x_scores"), sem("x_probs"), sem("x_used"), sem("x_ostep"), sem("x_odone"), sem("x_summed"), sem("x_normed"))
            mx_ready, mx_done, m_ready = sem("x_mxready"), sem("x_mxdone"), sem("x_mready")
            job_ready = [sem("x_job0"), sem("x_job1")]
            job_done = [sem("x_done0"), sem("x_done1")]
            k_high, q_high, k_twice, q_twice = sem("x_khigh"), sem("x_qhigh"), sem("x_ktwice"), sem("x_qtwice")
            block = ctx.enter_context(nc.Block())

            def wait_job(eng, job):
                i = place[job]
                eng.wait_ge(job_done[i % 2], i // 2 + 1)

            @block.sync
            def _(sp):
                sp.dma_start(self.bias[:, 0:C], a[names[4]].partition_broadcast(P)).then_inc(bo_in, 16)
                for p in range(pairs):
                    par = p % 2
                    sp.wait_ge(q_high, p + 1)
                    if p >= 2:
                        sp.wait_ge(sc_ready, 2 * KT * (p - 1))
                    sp.dma_start(raw(QB[0:DH, par, 0, :]), raw(QA[0:DH, par, 0, :])).then_inc(q_twice, 16)
                    sp.dma_start(raw(QB[0:DH, par, 1, :]), raw(QA[DH:P, par, 1, :])).then_inc(q_twice, 16)
                    sp.wait_ge(k_high, NC * (p + 1))
                    sp.dma_start(raw(KA[DH:P, par, 0, :]), raw(KA[0:DH, par, 0, :])).then_inc(k_twice, 16)
                    sp.dma_start(raw(KA[0:DH, par, 1, :]), raw(KA[DH:P, par, 1, :])).then_inc(k_twice, 16)
                if next_context is not None:
                    for g in (len(VG) - 2, len(VG) - 1):
                        wait_job(sp, ("v", pairs - 1, g))
                    self.load_context(sp, next_context)

            @block.gpsimd
            def _(pool):
                pool.wait_ge(bo_in, 16)
                for t in range(NT):
                    x = X[:, b * NT + t, :]
                    pool.tensor_tensor(x, x, self.bias[:, 0:C], ALU.add).then_inc(x_based, 1)
                for p in range(pairs):
                    if p >= 2:
                        i = place[("sum", p - 2, 0)]
                        pool.wait_ge(job_ready[i % 2], i // 2 + 1)
                    for t in range(1, KT):
                        for h in range(2):
                            n, r = TP * p + 2 * t + h, rows_of(t)
                            acc = ACC[0:r, p % 2, h, :]
                            pool.wait_ge(probs, n + 1)
                            if t >= 2:
                                pool.wait_ge(summed, sums_done(n) - 2)
                            other = acc if t >= 2 else PR[0:r, (n - 2) % RING, :]
                            pool.tensor_tensor(acc, other, PR[0:r, n % RING, :], ALU.add).then_inc(summed, 1)

            @block.tensor
            def _(pe):
                def job(x):
                    kind, p, c = x
                    i = place[x]
                    J = JB[i % 2]
                    if i >= 2:
                        pe.wait_ge(job_done[i % 2], i // 2)
                    if kind == "k":
                        o, w = CHUNKS[c]
                        pe.matmul(J[:, 0:w], wk[:, 0, p * P:(p + 1) * P], C0[:, o:o + w], start=True, stop=False)
                        last = pe.matmul(J[:, 0:w], wk[0:CC - P, 1, p * P:(p + 1) * P], C1[:, o:o + w], start=False, stop=True)
                    elif kind == "q":
                        for k in range(CK):
                            last = pe.matmul(J[:, :], wq[:, k, p * P:(p + 1) * P], HT[:, k, :], start=(k == 0), stop=(k == CK - 1))
                    elif kind == "v":
                        t0, n = VG[c]
                        for t in range(t0, t0 + n):
                            r, o = rows_of(t), (t - t0) * P
                            pe.matmul(J[0:r, o:o + P], C0[:, t * P:t * P + r], wv[:, 0, p * P:(p + 1) * P], start=True, stop=False)
                            last = pe.matmul(J[0:r, o:o + P], C1[:, t * P:t * P + r], wv[0:CC - P, 1, p * P:(p + 1) * P],
                                             start=False, stop=True)
                    elif kind == "row":
                        pe.wait_ge(m_ready, p + 1)
                        for t in range(NT):
                            last = pe.matmul(J[0:1, t * P:(t + 1) * P], m4[:, p % 2, t:t + 1], ident[:, :], start=True, stop=True)
                    elif kind == "sum":
                        pe.wait_ge(summed, 2 * (KT - 1) * (p + 1))
                        for h in range(2):
                            last = pe.matmul(J[h * DH:(h + 1) * DH, :], ones[:, 0:DH], ACC[:, p % 2, h, :], start=True, stop=True)
                    else:
                        pe.wait_ge(normed, p + 1)
                        for t in range(2):
                            q = 2 * c + t
                            last = pe.matmul(J[:, t * C:(t + 1) * C], OT[:, q * P:(q + 1) * P], wo[:, p, :], start=True, stop=True)
                    last.then_inc(job_ready[i % 2], 1)

                def maxima(j, i):
                    par, h, t, (o, w) = j // 2 % 2, j % 2, i // NC, CHUNKS[i % NC]
                    rows = slice(0, DH) if h == 0 else slice(DH, P)
                    m = NT * NC * j + i
                    if m >= 2:
                        pe.wait_ge(mx_done, m - 1)
                    pe.matmul(MB[m % 2][:, 0:w], QA[rows, par, h, t * P:(t + 1) * P], KA[rows, par, h, o:o + w],
                              start=True, stop=True).then_inc(mx_ready, 1)

                def maxima_inputs(j):
                    p = j // 2
                    wait_job(pe, ("q", p, 0))
                    wait_job(pe, ("k", p, NC - 2))
                    wait_job(pe, ("k", p, NC - 1))

                pe.wait_ge(self.ctx_in, 32 * ctx_loads)
                pe.wait_ge(self.xk_in, 32 * weight_loads)
                for x in before():
                    if x[0] == "k":
                        job(x)
                pe.wait_ge(self.xq_in, 16 * weight_loads)
                job(("q", 0, 0))
                pe.wait_ge(self.xv_in, 48 * weight_loads)
                maxima_inputs(0)
                for j in range(2):
                    for i in range(NT * NC):
                        maxima(j, i)
                        if (NT * NC * j + i) % 8 == 3:
                            job(("v", 0, (NT * NC * j + i) // 8))
                for x in first:
                    job(x)
                for p in range(pairs):
                    par = p % 2
                    for t in range(KT + 1):
                        for h in range(2 if t < KT else 0):
                            n, r = TP * p + 2 * t + h, rows_of(t)
                            if t == 0:
                                wait_job(pe, ("row", 2 * p + h, 0))
                                pe.wait_ge(q_twice, 32 * (p + 1))
                                pe.wait_ge(k_twice, 32 * (p + 1))
                            if n >= 3:
                                pe.wait_ge(probs, n - 2)
                            pe.matmul(SB[n % 3][0:r, :], KA[:, par, h, t * P:t * P + r], QA[:, par, h, :], start=True, stop=False)
                            pe.matmul(SB[n % 3][0:r, :], KB[:, par, h, t * P:t * P + r], QB[:, par, h, :],
                                      start=False, stop=True).then_inc(sc_ready, 1)
                            if t == 3 and h == 0 and p + 1 < pairs:
                                maxima_inputs(2 * p + 2)
                            for x in chunks_at(p, t)[h:h + 1]:
                                maxima(*x)
                        for x in at(p, t):
                            job(x)
                        for x in chunks_at(p, t)[2:3]:
                            maxima(*x)
                        if t >= 1:
                            s, r = t - 1, rows_of(t - 1)
                            n = TP * p + 2 * s
                            pe.wait_ge(probs, n + 2)
                            if p >= 1 and s == 0:
                                pe.wait_ge(o_done, p)
                            if s % NT == 0:
                                wait_job(pe, ("v", p, s // NT))
                            for h in range(2):
                                last = pe.matmul(OB[h * DH:(h + 1) * DH, :], V[0:r, par, s, h, :], PR[0:r, (n + h) % RING, :],
                                                 start=(s == 0), stop=(s == KT - 1))
                            last.then_inc(used, 1)
                        for x in chunks_at(p, t)[3:4]:
                            maxima(*x)
                for x in after:
                    job(x)

            @block.scalar
            def _(act):
                def job(x):
                    kind, p, c = x
                    i, par = place[x], p % 2
                    J = JB[i % 2]
                    if kind in ("out", "sum"):
                        return
                    act.wait_ge(job_ready[i % 2], i // 2 + 1)
                    if kind == "k":
                        o, w = CHUNKS[c]
                        if c == 0 and p >= 2:
                            act.wait_ge(sc_ready, 2 * KT * (p - 1))
                        act.activation(KA[0:DH, par, 0, o:o + w], J[0:DH, 0:w], ACT.Copy)
                        act.activation(KA[DH:P, par, 1, o:o + w], J[DH:P, 0:w], ACT.Copy).then_inc(k_high, 1)
                    elif kind == "q":
                        act.activation(QA[0:DH, par, 0, :], J[0:DH, :], ACT.Copy, scale=qscale[0:DH])
                        act.activation(QA[DH:P, par, 1, :], J[DH:P, :], ACT.Copy, scale=qscale[DH:P]).then_inc(q_high, 1)
                    elif kind == "v":
                        t0, n = VG[c]
                        if p >= 2:
                            act.wait_ge(used, KT * (p - 1))
                        r = rows_of(t0)
                        act.activation(V[0:r, par, t0:t0 + n, :, 0:DH].rearrange("p t h d -> p (t h) d"),
                                       J[0:r, 0:n * P].rearrange("p (th d) -> p th d", d=DH), ACT.Copy).then_inc(job_done[i % 2], 1)
                    elif kind == "row":
                        act.activation(QB[DH:DH + 1, p // 2 % 2, p % 2, :], J[0:1, :], ACT.Copy, scale=-1.0)\
                           .then_inc(job_done[i % 2], 1)

                def copy_outputs(p):
                    act.wait_ge(used, KT * (p + 1))
                    if p >= 1:
                        wait_job(act, ("out", p - 1, 0))
                        wait_job(act, ("out", p - 1, 1))
                    act.activation(OT, OB[:, :], ACT.Copy).then_inc(o_done, 1)

                for x in before():
                    if x[0] == "q":
                        act.wait_ge(prep, 1)
                    job(x)
                for x in first:
                    job(x)
                for p in range(pairs):
                    for t in range(KT + 1):
                        for h in range(2 if t < KT else 0):
                            n, r = TP * p + 2 * t + h, rows_of(t)
                            if n >= RING:
                                m = n - RING
                                act.wait_ge(used, KT * (m // TP) + m % TP // 2 + 1)
                                act.wait_ge(summed, sums_done(m))
                            act.wait_ge(sc_ready, n + 1)
                            act.activation(PR[0:r, n % RING, :], SB[n % 3][0:r, :], ACT.Exp,
                                           bias=keybias[0:r, t:t + 1] if masked else 0.0).then_inc(probs, 1)
                        if t == 0 and p >= 1:
                            copy_outputs(p - 1)
                        for x in at(p, t):
                            job(x)
                copy_outputs(pairs - 1)
                for x in after:
                    job(x)

            @block.vector
            def _(dve):
                steps = [0]

                def link(ins):
                    steps[0] += 1
                    ins.then_inc(o_step, 1)
                    dve.wait_ge(o_step, steps[0])

                def job(x):
                    kind, p, c = x
                    i, par = place[x], p % 2
                    J = JB[i % 2]
                    if kind == "k":
                        o, w = CHUNKS[c]
                        dve.wait_ge(k_high, NC * p + c + 1)
                        dve.tensor_tensor(KB[0:DH, par, 0, o:o + w], J[0:DH, 0:w], KA[0:DH, par, 0, o:o + w], ALU.subtract)
                        dve.tensor_tensor(KB[0:DH, par, 1, o:o + w], J[DH:P, 0:w], KA[DH:P, par, 1, o:o + w],
                                          ALU.subtract).then_inc(job_done[i % 2], 1)
                    elif kind == "q":
                        dve.wait_ge(q_high, p + 1)
                        dve.scalar_tensor_tensor(QA[DH:P, par, 0, :], J[0:DH, :], qscale[0:DH], QA[0:DH, par, 0, :],
                                                 ALU.mult, ALU.subtract)
                        dve.scalar_tensor_tensor(QA[0:DH, par, 1, :], J[DH:P, :], qscale[DH:P], QA[DH:P, par, 1, :],
                                                 ALU.mult, ALU.subtract).then_inc(job_done[i % 2], 1)
                    elif kind == "sum":
                        dve.wait_ge(job_ready[i % 2], i // 2 + 1)
                        if p >= 1:
                            dve.wait_ge(normed, p)
                        dve.reciprocal(RD, J[:, :]).then_inc(job_done[i % 2], 1)
                        wait_job(dve, x)
                        dve.wait_ge(o_done, p + 1)
                        dve.tensor_tensor(OT, OT, RD, ALU.mult).then_inc(normed, 1)
                    elif kind == "out":
                        dve.wait_ge(job_ready[i % 2], i // 2 + 1)
                        dve.wait_ge(x_based, NT)
                        x2 = X[:, b * NT + 2 * c:b * NT + 2 * c + 2, :]
                        dve.tensor_tensor(x2, J[:, :].rearrange("p (t n) -> p t n", t=2), x2, ALU.add)\
                           .then_inc(job_done[i % 2], 1)

                def maxima(j, i):
                    o, w = CHUNKS[i % NC]
                    w = min(w, S2 - o)
                    m = NT * NC * j + i
                    out = mx[:, j % 2, i // NC, i % NC:i % NC + 1]
                    dve.wait_ge(mx_ready, m + 1)
                    if masked:
                        dve.tensor_tensor_reduce(MB[m % 2][:, 0:w], MB[m % 2][:, 0:w], maskadd[:, o:o + w], 1.0, -BIG,
                                                 ALU.add, ALU.max, out).then_inc(mx_done, 1)
                    else:
                        dve.tensor_reduce(out, MB[m % 2][:, 0:w], AX.X, ALU.max).then_inc(mx_done, 1)

                def maxima_end(j):
                    dve.wait_ge(mx_done, NT * NC * (j + 1))
                    if j >= 2:
                        dve.wait_ge(job_ready[place[("row", j - 2, 0)] % 2], place[("row", j - 2, 0)] // 2 + 1)
                    dve.tensor_reduce(m4[:, j % 2, :], mx[:, j % 2, :, :], AX.X, ALU.max).then_inc(m_ready, 1)

                allowed, scale = self.small[:, 1:2], self.small[:, 2:3]

                def mask_step(c):
                    if not masked:
                        if c == 0:
                            dve.memset(qscale, DH ** -0.5).then_inc(prep, 1)
                        return
                    if c == 0:
                        dve.wait_ge(self.mask_in, 32 * mask_loads)
                        link(dve.tensor_copy(keybias, mask_cols))
                        link(dve.tensor_copy(maskadd, mask_rows))
                    elif c == 1:
                        link(dve.tensor_reduce(allowed, maskadd, AX.X, ALU.max))
                        link(dve.tensor_scalar(scale, allowed, BIG, None, ALU.mult))
                    elif c == 2:
                        link(dve.tensor_scalar(keybias, keybias, -1.0, scale, ALU.add, ALU.mult))
                        dve.tensor_scalar(qscale, allowed, DH ** -0.5, None, ALU.mult).then_inc(prep, 1)
                    else:
                        link(dve.tensor_scalar(maskadd, maskadd, -1.0, scale, ALU.add, ALU.mult))

                for x in before():
                    if x[0] == "q":
                        dve.wait_ge(prep, 1)
                    job(x)
                    if x[0] == "k":
                        mask_step(x[2])
                for j in range(2):
                    for i in range(NT * NC):
                        maxima(j, i)
                    maxima_end(j)
                for p in range(pairs):
                    for t in range(KT + 1):
                        for n, (j, i) in enumerate(chunks_at(p, t)):
                            if n == 2:
                                for x in at(p, t):
                                    job(x)
                            maxima(j, i)
                            if i == NT * NC - 1:
                                maxima_end(j)
                        if not chunks_at(p, t):
                            for x in at(p, t):
                                job(x)
                for x in after:
                    job(x)

    def top2(self, dve, link, logits, gates, exp_in, exp_out, to_exp, from_exp):
        rows, G = logits.shape[0], logits.shape[1]
        scratch = self.HTs[0:rows]
        n = G * E1 * E1
        more = scratch[:, 0:n].rearrange("p (g e j) -> p g e j", g=G, e=E1)
        same = scratch[:, n:2 * n].rearrange("p (g e j) -> p g e j", g=G, e=E1)
        rank = scratch[:, 2 * n:2 * n + G * E1].rearrange("p (g e) -> p g e", g=G)
        best = scratch[:, 2 * n + G * E1:2 * n + G * E1 + G]
        full = [rows, G, E1, E1]
        other = logits.unsqueeze(2).to_broadcast(full)
        own = logits.unsqueeze(3).to_broadcast(full)
        link(dve.tensor_tensor(more, other, own, ALU.is_gt))
        link(dve.tensor_tensor(same, other, own, ALU.is_equal))
        link(dve.tensor_tensor(same, same, self.tri[0:rows].unsqueeze(1).to_broadcast(full), ALU.mult))
        link(dve.tensor_tensor(more, more, same, ALU.add))
        link(dve.tensor_reduce(rank, more, AX.X, ALU.add))
        link(dve.tensor_scalar(rank, rank, 1.5, None, ALU.is_lt))
        link(dve.tensor_reduce(best, logits, AX.X, ALU.max))
        dve.tensor_tensor(exp_in, logits, best.unsqueeze(2).to_broadcast([rows, G, E1]), ALU.subtract).then_inc(to_exp, 1)
        dve.wait_ge(from_exp, 1)
        link(dve.tensor_tensor(gates, exp_out, rank, ALU.mult))
        link(dve.tensor_reduce(best, gates, AX.X, ALU.add))
        link(dve.reciprocal(best, best))
        link(dve.tensor_tensor(gates, gates, best.unsqueeze(2).to_broadcast([rows, G, E1]), ALU.mult))

    def mixture0(self, b):
        nc, a, HT, Hn, X, bank, W = self.nc, self.a, self.HT, self.Hn, self.X, self.bank, self.W
        KR = E0 * R0 // P
        wa = W[:, 0:KR * C].rearrange("p (k n) -> p k n", k=KR)
        wb = W[:, KR * C:2 * KR * C].rearrange("p (k n) -> p k n", k=KR)
        wr = W[:, 2048:2048 + CK * E0].rearrange("p (k n) -> p k n", k=CK)
        WB = W[:, 2560:2560 + CK * C].rearrange("p (k n) -> p k n", k=CK)
        logits = self.small[0:1, 32:40].rearrange("p (g e) -> p g e", g=1)
        gates = self.small[0:1, 40:48].rearrange("p (g e) -> p g e", g=1)
        exps = self.small[0:1, 48:64].rearrange("p (r g e) -> p r g e", r=2, g=1)
        gvec = self.small[:, 64:64 + KR]
        with self.stage() as (sem, ctx):
            w_in, lg_ready, to_exp, from_exp, step, g_ready, g_spread, b_scaled, wb_ready, wb_done, y_ready, based = (
                sem("e_w"), sem("e_lg"), sem("e_toexp"), sem("e_fromexp"), sem("e_step"), sem("e_gready"),
                sem("e_gspread"), sem("e_bscaled"), sem("e_wbready"), sem("e_wbdone"), sem("e_y"), sem("e_based"))
            block = ctx.enter_context(nc.Block())

            @block.sync
            def _(sp):
                sp.dma_start(wr, a["wr0T"].rearrange("(k p) e -> p k e", p=P)).then_inc(w_in, 16)
                sp.dma_start(wa, a["A0"].rearrange("(k p) n -> p k n", p=P)).then_inc(w_in, 16)
                sp.dma_start(wb, a["B0T"].rearrange("(k p) n -> p k n", p=P)).then_inc(w_in, 16)

            @block.gpsimd
            def _(pool):
                for t in range(NT):
                    x = X[:, b * NT + t, :]
                    pool.tensor_tensor(x, x, Hn[:, t, :], ALU.add).then_inc(based, 1)

            @block.tensor
            def _(pe):
                pe.wait_ge(w_in, 48)
                for k in range(CK):
                    last = pe.matmul(bank[0][0:1, 0:E0], HT[:, k, 0:1], wr[:, k, :], start=(k == 0), stop=(k == CK - 1))
                last.then_inc(lg_ready, 1)
                pe.wait_ge(g_ready, 1)
                pe.matmul(bank[1][:, 0:E0], self.ones[0:1, :], gates[0:1, 0, :], start=True, stop=True).then_inc(g_spread, 1)
                pe.wait_ge(b_scaled, KR)
                for m in range(CK):
                    for k in range(KR):
                        last = pe.matmul(bank[2][:, m * C:(m + 1) * C], wa[:, k, m * P:(m + 1) * P], wb[:, k, :],
                                         start=(k == 0), stop=(k == KR - 1))
                last.then_inc(wb_ready, 1)
                pe.wait_ge(wb_done, 1)
                for t in range(NT):
                    for k in range(CK):
                        last = pe.matmul(bank[3 + t][:, 0:C], HT[:, k, t * P:(t + 1) * P], WB[:, k, :],
                                         start=(k == 0), stop=(k == CK - 1))
                    last.then_inc(y_ready, 1)

            @block.scalar
            def _(act):
                act.wait_ge(to_exp, 1)
                act.activation(exps[:, 1], exps[:, 0], ACT.Exp).then_inc(from_exp, 1)
                act.wait_ge(wb_ready, 1)
                act.activation(WB, bank[2][:, :].rearrange("p (k n) -> p k n", k=CK), ACT.Copy).then_inc(wb_done, 1)

            @block.vector
            def _(dve):
                steps = [0]

                def link(ins):
                    steps[0] += 1
                    ins.then_inc(step, 1)
                    dve.wait_ge(step, steps[0])

                dve.wait_ge(lg_ready, 1)
                link(dve.tensor_copy(logits[:, 0, :], bank[0][0:1, 0:E0]))
                self.top2(dve, link, logits, gates, exps[:, 0], exps[:, 1], to_exp, from_exp)
                dve.tensor_copy(gvec[0:1, 0:1], gates[0:1, 0, 0:1]).then_inc(g_ready, 1)
                dve.wait_ge(g_spread, 1)
                dve.wait_ge(g_ready, 1)
                dve.tensor_copy(gvec[0:R0], bank[1][0:R0, 0:E0:2]).then_inc(step, 1)
                dve.tensor_copy(gvec[R0:P], bank[1][R0:P, 1:E0:2]).then_inc(step, 1)
                steps[0] += 2
                dve.wait_ge(step, steps[0])
                dve.wait_ge(w_in, 48)
                for k in range(KR):
                    dve.tensor_scalar(wb[:, k, :], wb[:, k, :], gvec[:, k:k + 1], None, ALU.mult).then_inc(b_scaled, 1)
                dve.wait_ge(based, NT)
                for t in range(NT):
                    x = X[:, b * NT + t, :]
                    dve.wait_ge(y_ready, t + 1)
                    dve.tensor_tensor(x, bank[3 + t][:, 0:C], x, ALU.add).then_inc(step, 1)

    def attention1(self, b):
        nc, a, HT, bank, W = self.nc, self.a, self.HT, self.bank, self.W
        w = W[:, 0:CK * 3 * C].rearrange("p (k n) -> p k n", k=CK)
        bias = W[:, 1536:1536 + 3 * C]
        gamma = W[:, 2304:2304 + 3 * C]
        alpha = self.bias[:, 0:C]
        Kb = [W[:, 4096 + 1024 * i:5120 + 1024 * i] for i in range(B)]
        vflat = self.V[:, :, :, :, :].rearrange("p a k h d -> p (a k h d)")
        Vb = [vflat[:, 1024 * i:1024 * (i + 1)] for i in range(3)] + [self.C0[:, 0:1024]]
        q1 = self.ACC[:, 0, :, :].rearrange("p h n -> p (h n)")
        prod = [self.PR[:, 2 * i:2 * i + 2, :].rearrange("p r n -> p (r n)") for i in range(2)]
        A = self.Hn[:, :, :].rearrange("p t n -> p (t n)")
        R = NT * H
        sc = self.small[:, 0:R * B].rearrange("p (r s) -> p r s", s=B)[:, :, 0:b + 1]
        pr = self.small[:, R * B:2 * R * B - R].rearrange("p (r s) -> p r s", s=B - 1)
        m = self.bias[:, 512:512 + R]
        full = [P, R, b + 1]
        with self.stage() as (sem, ctx):
            w_in, b_in, y_ready, step, to_exp, from_exp = (
                sem("t_w"), sem("t_b"), sem("t_y"), sem("t_step"), sem("t_toexp"), sem("t_fromexp"))
            block = ctx.enter_context(nc.Block())

            @block.sync
            def _(sp):
                sp.dma_start(w, a["w1_in"].rearrange("(k p) n -> p k n", p=P)).then_inc(w_in, 16)
                sp.dma_start(bias, a["b1_in"].partition_broadcast(P)).then_inc(b_in, 16)
                sp.dma_start(gamma, a["gamma1"].partition_broadcast(P)).then_inc(b_in, 16)
                sp.dma_start(alpha, a["alpha1"].partition_broadcast(P)).then_inc(b_in, 16)

            @block.tensor
            def _(pe):
                pe.wait_ge(w_in, 16)
                for t in range(NT):
                    for o, n, J in ((0, 2 * C, bank[2 * t]), (2 * C, C, bank[2 * t + 1])):
                        for k in range(CK):
                            last = pe.matmul(J[:, 0:n], HT[:, k, t * P:(t + 1) * P], w[:, k, o:o + n],
                                             start=(k == 0), stop=(k == CK - 1))
                    last.then_inc(y_ready, 1)

            @block.scalar
            def _(act):
                act.wait_ge(to_exp, 1)
                act.activation(sc, sc, ACT.Exp, scale=D ** -0.5).then_inc(from_exp, 1)

            @block.vector
            def _(dve):
                steps = [0]

                def done(ins):
                    steps[0] += 1
                    ins.then_inc(step, 1)

                def link(ins):
                    done(ins)
                    dve.wait_ge(step, steps[0])

                dve.wait_ge(b_in, 48)
                for t in range(NT):
                    dve.wait_ge(y_ready, t + 1)
                    parts = [(q1, bank[2 * t][:, 0:C], 0), (Kb[b], bank[2 * t][:, C:2 * C], C), (Vb[b], bank[2 * t + 1][:, 0:C], 2 * C)]
                    for dst, src, o in parts:
                        done(dve.tensor_tensor(dst[:, t * C:(t + 1) * C], src, bias[:, o:o + C], ALU.add))
                    dve.wait_ge(step, steps[0])
                    for dst, _, o in parts:
                        d = dst[:, t * C:(t + 1) * C]
                        done(dve.tensor_tensor(d, d, gamma[:, o:o + C], ALU.mult))
                dve.wait_ge(step, steps[0])
                for s in range(b + 1):
                    link(dve.tensor_tensor(prod[s % 2], q1, Kb[s], ALU.mult))
                    done(dve.tensor_reduce(sc[:, :, s:s + 1].rearrange("p r o -> p (r o)"),
                                           prod[s % 2].rearrange("p (r d) -> p r d", d=D), AX.X, ALU.add))
                dve.wait_ge(step, steps[0])
                link(dve.tensor_reduce(m, sc, AX.X, ALU.max))
                dve.tensor_tensor(sc, sc, m.unsqueeze(2).to_broadcast(full), ALU.subtract).then_inc(to_exp, 1)
                dve.wait_ge(from_exp, 1)
                link(dve.tensor_reduce(m, sc, AX.X, ALU.add))
                link(dve.reciprocal(m, m))
                link(dve.tensor_tensor(sc, sc, m.unsqueeze(2).to_broadcast(full), ALU.mult))
                for s in range(b + 1):
                    dst = A if s == 0 else prod[s % 2]
                    link(dve.tensor_tensor(dst.rearrange("p (r d) -> p r d", d=D), Vb[s].rearrange("p (r d) -> p r d", d=D),
                                           sc[:, :, s].unsqueeze(2).to_broadcast([P, R, D]), ALU.mult))
                    if s > 0:
                        link(dve.tensor_tensor(A, A, dst, ALU.add))
                done(dve.tensor_tensor(self.Hn[:, :, :], self.Hn[:, :, :], alpha.unsqueeze(1).to_broadcast([P, NT, C]), ALU.mult))

    def expert_products(self):
        nc, a, bank, W = self.nc, self.a, self.bank, self.W
        KF = F1 // P
        WE = W[:, 0:CK * E1 * C].rearrange("p (k e n) -> p k e n", k=CK, e=E1)
        vflat = self.V[:, :, :, :, :].rearrange("p a k h d -> p (a k h d)")
        pflat = self.PR[:, 0:4, :].rearrange("p r n -> p (r n)")
        first = [W[:, 4096:6144], vflat[:, 0:2048]]
        second = [W[:, 6144:8192], pflat]
        first, second = ([x.rearrange("p (k n) -> p k n", k=KF) for x in y] for y in (first, second))
        with self.stage() as (sem, ctx):
            in0, in1, ready, taken = sem("w_in0"), sem("w_in1"), sem("w_ready"), sem("w_taken")
            block = ctx.enter_context(nc.Block())

            @block.sync
            def _(sp):
                for e in range(E1):
                    if e >= 2:
                        sp.wait_ge(ready, e - 1)
                    sp.dma_start(first[e % 2], a["w_in1"][e].rearrange("(k p) n -> p k n", p=P)).then_inc((in0, in1)[e % 2], 16)
                    sp.dma_start(second[e % 2], a["w_out1T"][e].rearrange("(k p) n -> p k n", p=P)).then_inc((in0, in1)[e % 2], 16)

            @block.tensor
            def _(pe):
                for e in range(E1):
                    pe.wait_ge((in0, in1)[e % 2], 32 * (e // 2 + 1))
                    if e >= 2:
                        pe.wait_ge(taken, e - 1)
                    for m in range(CK):
                        for k in range(KF):
                            last = pe.matmul(bank[e % 2][:, m * C:(m + 1) * C], first[e % 2][:, k, m * P:(m + 1) * P],
                                             second[e % 2][:, k, :], start=(k == 0), stop=(k == KF - 1))
                    last.then_inc(ready, 1)

            @block.scalar
            def _(act):
                for e in range(E1):
                    act.wait_ge(ready, e + 1)
                    act.activation(WE[:, :, e, :], bank[e % 2][:, :].rearrange("p (k n) -> p k n", k=CK), ACT.Copy).then_inc(taken, 1)

    def mixture1(self, b):
        nc, a, HT, X, bank, W = self.nc, self.a, self.HT, self.X, self.bank, self.W
        WE = W[:, 0:CK * E1 * C].rearrange("p (k n) -> p k n", k=CK)
        wg = self.bias[:, 0:CK * E1].rearrange("p (k n) -> p k n", k=CK)
        G = NT * E1
        logits, gates, ein, eout = (self.small[:, G * i:G * (i + 1)].rearrange("p (g e) -> p g e", g=NT) for i in range(4))
        YB = bank[2:6]
        with self.stage() as (sem, ctx):
            w_in, lg_ready, to_exp, from_exp, step, y_ready, y_done = (
                sem("g_w"), sem("g_lg"), sem("g_toexp"), sem("g_fromexp"), sem("g_step"), sem("g_y"), sem("g_ydone"))
            block = ctx.enter_context(nc.Block())

            @block.sync
            def _(sp):
                sp.dma_start(wg, a["wg1T"].rearrange("(k p) e -> p k e", p=P)).then_inc(w_in, 16)

            @block.tensor
            def _(pe):
                pe.wait_ge(w_in, 16)
                for t in range(NT):
                    for k in range(CK):
                        last = pe.matmul(bank[0][:, t * E1:(t + 1) * E1], HT[:, k, t * P:(t + 1) * P], wg[:, k, :],
                                         start=(k == 0), stop=(k == CK - 1))
                last.then_inc(lg_ready, 1)
                for n in range(NT * E1 // 2):
                    t, e2 = n % NT, n // NT
                    if n >= 4:
                        pe.wait_ge(y_done, 2 * (n - 3))
                    for k in range(CK):
                        last = pe.matmul(YB[n % 4][:, :], HT[:, k, t * P:(t + 1) * P], WE[:, k, 2 * C * e2:2 * C * (e2 + 1)],
                                         start=(k == 0), stop=(k == CK - 1))
                    last.then_inc(y_ready, 1)

            @block.scalar
            def _(act):
                act.wait_ge(to_exp, 1)
                act.activation(eout, ein, ACT.Exp).then_inc(from_exp, 1)

            @block.vector
            def _(dve):
                steps = [0]

                def link(ins):
                    steps[0] += 1
                    ins.then_inc(step, 1)
                    dve.wait_ge(step, steps[0])

                dve.wait_ge(lg_ready, 1)
                link(dve.tensor_copy(logits, bank[0][:, 0:G].rearrange("p (g e) -> p g e", g=NT)))
                self.top2(dve, link, logits, gates, ein, eout, to_exp, from_exp)
                n = 0
                for e2 in range(E1 // 2):
                    for t in range(NT):
                        x = X[:, b * NT + t, :]
                        for h in range(2):
                            e = 2 * e2 + h
                            if h == 0:
                                dve.wait_ge(y_ready, n // 2 + 1)
                                if n >= 2 * NT:
                                    dve.wait_ge(y_done, n - 2 * NT + 2)
                            else:
                                dve.wait_ge(y_done, n)
                            dve.scalar_tensor_tensor(x, YB[n // 2 % 4][:, h * C:(h + 1) * C], gates[:, t, e:e + 1], x,
                                                     ALU.mult, ALU.add).then_inc(y_done, 1)
                            n += 1

    def run(self):
        cross0, cross1 = ("xq0", "xk0", "xv0", "xo0", "xb0"), ("xq1", "xk1", "xv1", "xo1", "xb1")
        self.load_inputs()
        self.cross_constants()
        for b in range(B):
            self.norm(b)
            self.self_project(b)
            self.self_attend(b)
            self.project_out(b, self.a["w0_out"], self.a["b0_out"], ahead=(b, 8, cross0, True))
            self.norm(b)
            self.cross_attention(b, 8, cross0, True)
            self.norm(b)
            self.mixture0(b)
        for b in range(B):
            self.norm(b)
            self.attention1(b)
            self.project_out(b, self.a["w1_out"], self.a["b1_out"], self.a["gamma2"],
                             ahead=(0, 16, cross1, False) if b == B - 1 else None)
        for b in range(B):
            self.norm(b)
            self.cross_attention(b, 16, cross1, False, next_context=b + 1 if b + 1 < B else None)
        self.expert_products()
        for b in range(B):
            self.norm(b)
            self.mixture1(b)
        self.store_outputs()


def layouts(i):
    import numpy as np
    g = {k: np.asarray(v) for k, v in i.items()}

    def flat(name):
        return g[name].reshape(-1)

    mask = g["mask_BxS2_bk0"]
    padded = np.zeros((B, KT * P), mask.dtype)
    padded[:, :S2] = mask
    out = {
        "x": g["x"], "ctxT": g["ctx_768"].transpose(0, 2, 1),
        "mask": mask, "maskT": padded.reshape(B, KT, P).transpose(0, 2, 1),
        "w0_in": g["L0_attn_in_proj_weight"].T, "b0_in": g["L0_attn_in_proj_bias"],
        "b0_cols": g["L0_attn_in_proj_bias"][0:2 * C].reshape(4, P).T,
        "w0_out": g["L0_attn_out_proj_weight"].T, "b0_out": g["L0_attn_out_proj_bias"],
        "xq0": g["L0_xattn_W_q"], "xk0": g["L0_xattn_W_k"], "xv0": g["L0_xattn_W_v"], "xo0": g["L0_xattn_W_o"],
        "xb0": g["L0_xattn_b_o"],
        "wr0T": g["L0_ffn_Wr"].T, "A0": g["L0_ffn_A"].reshape(E0 * R0, C),
        "B0T": g["L0_ffn_Bw"].transpose(0, 2, 1).reshape(E0 * R0, C),
        "w1_in": g["L1_attn_in_proj_weight"].T, "b1_in": g["L1_attn_in_proj_bias"],
        "gamma1": flat("L1_attn_gamma"), "alpha1": flat("L1_attn_linear_alpha"), "gamma2": flat("L1_attn_linear_gamma"),
        "w1_out": g["L1_attn_out_proj_weight"].T, "b1_out": g["L1_attn_out_proj_bias"],
        "xq1": g["L1_xattn_Wq"], "xk1": g["L1_xattn_Wk"], "xv1": g["L1_xattn_Wv"], "xo1": g["L1_xattn_Wo"],
        "xb1": g["L1_xattn_bo"],
        "wg1T": g["L1_ffn_w_gate"].T, "w_in1": g["L1_ffn_w_in"], "w_out1T": g["L1_ffn_w_out"].transpose(0, 2, 1),
    }
    return {k: np.ascontiguousarray(v) for k, v in out.items()}


def kernel(**inputs):
    import concourse.bacc as _bacc
    from concourse.bass_utils import run_bass_kernel_spmd as _run

    nc = _bacc.Bacc("TRN2", target_bir_lowering=False, num_devices=1)
    arrays = layouts(inputs)
    aps = {k: nc.dram_tensor(f"in_{k}", v.shape, mybir.dt.from_np(v.dtype), kind="ExternalInput").ap()
           for k, v in arrays.items()}
    out = nc.dram_tensor("out_x", (B, S, C), F32, kind="ExternalOutput").ap()
    with ExitStack() as ctx:
        Core(nc, ctx, aps, out).run()
    r = _run(nc, [{f"in_{k}": v for k, v in arrays.items()}], core_ids=[0])
    return r.results[0]["out_x"]
```
